# Optimizing a Trainium2 kernel written in Bass

```python
import numpy as np
import jax
import jax.numpy as jnp

def _softmax(x, axis=-1):
    return jax.nn.softmax(x, axis=axis)

def _gelu(x):
    return jax.nn.gelu(x, approximate=True)

def _silu(x):
    return jax.nn.silu(x)

def _sigmoid(x):
    return jax.nn.sigmoid(x)

def _layernorm(x, axis=-1, eps=1e-05):
    m = jnp.mean(x, axis=axis, keepdims=True)
    v = jnp.var(x, axis=axis, keepdims=True)
    return (x - m) / jnp.sqrt(v + eps)

def _scatter_add(tgt, idx, src, axis=0):
    return tgt.at[idx].add(src)

def _segment_sum(src, seg, n):
    return jax.ops.segment_sum(src, seg, n)
kernel_name = 'mk_xattn_ffn_d2_seqx_r8_2a8dde'

def setup_inputs(seed: int=0):
    np.random.seed(seed)
    _w = jnp.asarray

    def _rec_inputs():
        import jax
        import jax.numpy as jnp
        _rk = jax.random.key(seed)
        x = -0.000125 + 0.9999 * jax.random.normal(jax.random.fold_in(_rk, 1), (2, 512, 128), jnp.float32)
        _lenS = 512 - jax.random.randint(jax.random.fold_in(_rk, 7), (2,), 0, max(1, 512 // 4) + 1, jnp.int32)
        _lenS2 = 154 - jax.random.randint(jax.random.fold_in(_rk, 8), (2,), 0, max(1, 154 // 4) + 1, jnp.int32)
        _ctx_1024P = jax.random.normal(jax.random.fold_in(_rk, 11), (2, 16, 128), jnp.float32)
        _ctx_1024c = jax.random.dirichlet(jax.random.fold_in(_rk, 511), 0.3 * jnp.ones((16,), jnp.float32), (2, 154))
        _ctx_1024t = jnp.einsum('bsk,bkd->bsd', _ctx_1024c, _ctx_1024P)
        _ctx_1024t = _ctx_1024t * jax.lax.rsqrt(jnp.mean(jnp.square(_ctx_1024t)) + 1e-12) * 0.953939
        ctx_1024 = -1.52775e-05 + 0.999936 * (_ctx_1024t + 0.3 * jax.random.normal(jax.random.fold_in(_rk, 611), (2, 154, 128), jnp.float32))
        _validS = jnp.arange(512)[None, :] < _lenS[:, None]
        _validS2 = jnp.arange(154)[None, :] < _lenS2[:, None]
        _causal = jnp.tril(jnp.ones((512, 512), dtype=bool))
        mask_BxS2_bk0 = jnp.logical_not(jnp.broadcast_to(_validS2[:, :], (2, 154)))
        return (x, ctx_1024, mask_BxS2_bk0)
    x, ctx_1024, mask_BxS2_bk0 = _rec_inputs()

    def _L0_xattn_setup():
        import jax, jax.numpy as jnp
        import numpy as np
        DIM = 128
        EPS_DENOM = 1e-06
        EPS_LN = 1e-05

        def _layernorm(x, gamma, beta):
            mu = jnp.mean(x, axis=-1, keepdims=True)
            var = jnp.var(x, axis=-1, keepdims=True)
            return (x - mu) * jax.lax.rsqrt(var + EPS_LN) * gamma + beta
        key = jax.random.key(seed)
        ks = jax.random.split(key, 12)
        B, T, D = (8, 512, DIM)
        s = 1.0 / np.sqrt(D)
        return {'audio': jax.random.normal(ks[0], (B, T, D), jnp.float32), 'video': jax.random.normal(ks[1], (B, T, D), jnp.float32), 'Wq': jax.random.normal(ks[2], (D, D), jnp.float32) * s, 'bq': jax.random.normal(ks[3], (D,), jnp.float32) * 0.02, 'Wk': jax.random.normal(ks[4], (D, D), jnp.float32) * s, 'bk': jax.random.normal(ks[5], (D,), jnp.float32) * 0.02, 'Wv': jax.random.normal(ks[6], (D, D), jnp.float32) * s, 'bv': jax.random.normal(ks[7], (D,), jnp.float32) * 0.02, 'Wo': jax.random.normal(ks[8], (D, D), jnp.float32) * s, 'bo': jax.random.normal(ks[9], (D,), jnp.float32) * 0.02, 'gamma': jnp.ones((D,), jnp.float32), 'beta': jnp.zeros((D,), jnp.float32)}
    _L0_xattn_all = _L0_xattn_setup()
    _L0_xattn_in = {k: v for k, v in _L0_xattn_all.items() if k in ('Wq', 'bq', 'Wk', 'bk', 'Wv', 'bv', 'Wo', 'bo', 'gamma', 'beta')}
    del _L0_xattn_all

    def _L0_ffn_setup():
        import jax, jax.numpy as jnp
        import numpy as np
        from jax import lax
        T, B, I, M, O = (32, 64, 128, 128, 128)

        def _xavier(key, shape):
            fan_out, fan_in = shape
            limit = float(np.sqrt(6.0 / (fan_in + fan_out)))
            return jax.random.uniform(key, shape, jnp.float32, -limit, limit)
        key = jax.random.key(seed)
        ks = jax.random.split(key, 9)
        x = jax.random.normal(ks[0], (T, B, I), jnp.float32)
        return {'x': x, 'wf': _xavier(ks[1], (M, I)), 'uf': _xavier(ks[2], (M, M)), 'bf': jnp.zeros((M,), jnp.float32), 'wi': _xavier(ks[3], (M, I)), 'ui': _xavier(ks[4], (M, M)), 'bi': jnp.zeros((M,), jnp.float32), 'wc': _xavier(ks[5], (M, I)), 'uc': _xavier(ks[6], (M, M)), 'bc': jnp.zeros((M,), jnp.float32), 'wo': _xavier(ks[7], (O, I)), 'uo': _xavier(ks[8], (O, M)), 'bo': jnp.zeros((O,), jnp.float32), 'in_c': jnp.zeros((M,), jnp.float32)}
    _L0_ffn_all = _L0_ffn_setup()
    _L0_ffn_in = {k: v for k, v in _L0_ffn_all.items() if k in ('wf', 'uf', 'bf', 'wi', 'ui', 'bi', 'wc', 'uc', 'bc', 'wo', 'uo', 'bo', 'in_c')}
    del _L0_ffn_all

    def _L1_xattn_setup():
        import jax, jax.numpy as jnp
        import numpy as np
        B, TQ, TK, D, H = (2, 256, 256, 128, 16)
        HD = D // H
        NUM_PAD = 32
        key = jax.random.key(seed)
        ks = jax.random.split(key, 8)
        s = 0.02
        q = jax.random.normal(ks[0], (B, TQ, D), dtype=jnp.float32)
        kv = jax.random.normal(ks[1], (B, TK, D), dtype=jnp.float32)
        key_padding_mask = jnp.broadcast_to(jnp.arange(TK) >= TK - NUM_PAD, (B, TK))
        Wq = jax.random.normal(ks[2], (D, D), dtype=jnp.float32) * s
        bq = jax.random.normal(ks[3], (D,), dtype=jnp.float32) * s
        Wkv = jax.random.normal(ks[4], (D, 2 * D), dtype=jnp.float32) * s
        bkv = jax.random.normal(ks[5], (2 * D,), dtype=jnp.float32) * s
        Wo = jax.random.normal(ks[6], (D, D), dtype=jnp.float32) * s
        bo = jax.random.normal(ks[7], (D,), dtype=jnp.float32) * s
        return {'q': q, 'kv': kv, 'key_padding_mask': key_padding_mask, 'Wq': Wq, 'bq': bq, 'Wkv': Wkv, 'bkv': bkv, 'Wo': Wo, 'bo': bo}
    _L1_xattn_all = _L1_xattn_setup()
    _L1_xattn_in = {k: v for k, v in _L1_xattn_all.items() if k in ('Wq', 'bq', 'Wkv', 'bkv', 'Wo', 'bo')}
    del _L1_xattn_all

    def _L1_ffn_setup():
        import jax, jax.numpy as jnp
        import numpy as np
        D_MODEL = 128
        NUM_EXPERTS = 8
        TOP_K = 2
        B, S = (4, 256)
        key = jax.random.key(seed)
        ks = jax.random.split(key, 7)
        scale_in = 1.0 / np.sqrt(D_MODEL)
        scale_hid = 1.0 / np.sqrt(2 * D_MODEL)
        return {'x': jax.random.normal(ks[0], (B, S, D_MODEL), dtype=jnp.float32), 'Wg': jax.random.normal(ks[1], (D_MODEL, NUM_EXPERTS), dtype=jnp.float32) * scale_in, 'bg': jnp.zeros((NUM_EXPERTS,), dtype=jnp.float32), 'W1': jax.random.normal(ks[2], (NUM_EXPERTS, D_MODEL, 2 * D_MODEL), dtype=jnp.float32) * scale_in, 'b1': jnp.zeros((NUM_EXPERTS, 2 * D_MODEL), dtype=jnp.float32), 'W2': jax.random.normal(ks[3], (NUM_EXPERTS, 2 * D_MODEL, D_MODEL), dtype=jnp.float32) * scale_hid, 'b2': jnp.zeros((NUM_EXPERTS, D_MODEL), dtype=jnp.float32)}
    _L1_ffn_all = _L1_ffn_setup()
    _L1_ffn_in = {k: v for k, v in _L1_ffn_all.items() if k in ('Wg', 'bg', 'W1', 'b1', 'W2', 'b2')}
    del _L1_ffn_all
    return {'x': x, 'ctx_1024': ctx_1024, 'mask_BxS2_bk0': mask_BxS2_bk0, 'L0_xattn_Wq': _L0_xattn_in['Wq'], 'L0_xattn_bq': _L0_xattn_in['bq'], 'L0_xattn_Wk': _L0_xattn_in['Wk'], 'L0_xattn_bk': _L0_xattn_in['bk'], 'L0_xattn_Wv': _L0_xattn_in['Wv'], 'L0_xattn_bv': _L0_xattn_in['bv'], 'L0_xattn_Wo': _L0_xattn_in['Wo'], 'L0_xattn_bo': _L0_xattn_in['bo'], 'L0_xattn_gamma': _L0_xattn_in['gamma'], 'L0_xattn_beta': _L0_xattn_in['beta'], 'L0_ffn_wf': _L0_ffn_in['wf'], 'L0_ffn_uf': _L0_ffn_in['uf'], 'L0_ffn_bf': _L0_ffn_in['bf'], 'L0_ffn_wi': _L0_ffn_in['wi'], 'L0_ffn_ui': _L0_ffn_in['ui'], 'L0_ffn_bi': _L0_ffn_in['bi'], 'L0_ffn_wc': _L0_ffn_in['wc'], 'L0_ffn_uc': _L0_ffn_in['uc'], 'L0_ffn_bc': _L0_ffn_in['bc'], 'L0_ffn_wo': _L0_ffn_in['wo'], 'L0_ffn_uo': _L0_ffn_in['uo'], 'L0_ffn_bo': _L0_ffn_in['bo'], 'L0_ffn_in_c': _L0_ffn_in['in_c'], 'L1_xattn_Wq': _L1_xattn_in['Wq'], 'L1_xattn_bq': _L1_xattn_in['bq'], 'L1_xattn_Wkv': _L1_xattn_in['Wkv'], 'L1_xattn_bkv': _L1_xattn_in['bkv'], 'L1_xattn_Wo': _L1_xattn_in['Wo'], 'L1_xattn_bo': _L1_xattn_in['bo'], 'L1_ffn_Wg': _L1_ffn_in['Wg'], 'L1_ffn_bg': _L1_ffn_in['bg'], 'L1_ffn_W1': _L1_ffn_in['W1'], 'L1_ffn_b1': _L1_ffn_in['b1'], 'L1_ffn_W2': _L1_ffn_in['W2'], 'L1_ffn_b2': _L1_ffn_in['b2']}

def reference(x, ctx_1024, mask_BxS2_bk0, L0_xattn_Wq, L0_xattn_bq, L0_xattn_Wk, L0_xattn_bk, L0_xattn_Wv, L0_xattn_bv, L0_xattn_Wo, L0_xattn_bo, L0_xattn_gamma, L0_xattn_beta, L0_ffn_wf, L0_ffn_uf, L0_ffn_bf, L0_ffn_wi, L0_ffn_ui, L0_ffn_bi, L0_ffn_wc, L0_ffn_uc, L0_ffn_bc, L0_ffn_wo, L0_ffn_uo, L0_ffn_bo, L0_ffn_in_c, L1_xattn_Wq, L1_xattn_bq, L1_xattn_Wkv, L1_xattn_bkv, L1_xattn_Wo, L1_xattn_bo, L1_ffn_Wg, L1_ffn_bg, L1_ffn_W1, L1_ffn_b1, L1_ffn_W2, L1_ffn_b2):
    import jax
    import jax.numpy as jnp

    def _L0_xattn_ref(audio, video, Wq, bq, Wk, bk, Wv, bv, Wo, bo, gamma, beta):
        import jax, jax.numpy as jnp
        import numpy as np
        DIM = 128
        EPS_DENOM = 1e-06
        EPS_LN = 1e-05

        def _layernorm(x, gamma, beta):
            mu = jnp.mean(x, axis=-1, keepdims=True)
            var = jnp.var(x, axis=-1, keepdims=True)
            return (x - mu) * jax.lax.rsqrt(var + EPS_LN) * gamma + beta
        Q = audio @ Wq.T + bq
        K = video @ Wk.T + bk
        V = video @ Wv.T + bv
        Q = jax.nn.elu(Q) + 1.0
        K = jax.nn.elu(K) + 1.0
        KV = jnp.einsum('btd,bte->bde', K, V)
        K_sum = K.sum(axis=1)
        attn_num = jnp.einsum('btd,bde->bte', Q, KV)
        attn_denom = Q * K_sum[:, None, :] + EPS_DENOM
        attn_out = attn_num / attn_denom
        attn_out = attn_out @ Wo.T + bo
        return _layernorm(audio + attn_out, gamma, beta)

    def _L0_ffn_ref(x, wf, uf, bf, wi, ui, bi, wc, uc, bc, wo, uo, bo, in_c):
        import jax, jax.numpy as jnp
        import numpy as np
        from jax import lax
        T, B, I, M, O = (32, 64, 128, 128, 128)

        def _xavier(key, shape):
            fan_out, fan_in = shape
            limit = float(np.sqrt(6.0 / (fan_in + fan_out)))
            return jax.random.uniform(key, shape, jnp.float32, -limit, limit)
        batch = x.shape[1]
        c0 = jnp.broadcast_to(in_c, (batch, in_c.shape[0]))

        def step(c, xt):
            ft = jax.nn.sigmoid(xt @ wf.T + c @ uf.T + bf)
            it = jax.nn.sigmoid(xt @ wi.T + c @ ui.T + bi)
            gt = jnp.tanh(xt @ wc.T + c @ uc.T + bc)
            c = ft * c + it * gt
            return (c, None)
        c_final, _ = lax.scan(step, c0, x)
        h = jnp.tanh(jnp.einsum('tbi,oi->tbo', x, wo) + c_final @ uo.T + bo)
        return h

    def _L1_xattn_ref(q, kv, key_padding_mask, Wq, bq, Wkv, bkv, Wo, bo):
        import jax, jax.numpy as jnp
        import numpy as np
        B, TQ, TK, D, H = (2, 256, 256, 128, 16)
        HD = D // H
        NUM_PAD = 32
        Bc, Tq, Dm = q.shape
        Tk = kv.shape[1]
        scale = HD ** (-0.5)
        Q = (q @ Wq + bq).reshape(Bc, Tq, H, HD).transpose(0, 2, 1, 3)
        KV = (kv @ Wkv + bkv).reshape(Bc, Tk, 2, H, HD).transpose(2, 0, 3, 1, 4)
        K, V = (KV[0], KV[1])
        attn = jnp.einsum('bhqd,bhkd->bhqk', Q, K) * scale
        attn = jnp.where(key_padding_mask[:, None, None, :], -jnp.inf, attn)
        attn = jax.nn.softmax(attn, axis=-1)
        out = jnp.einsum('bhqk,bhkd->bhqd', attn, V)
        out = out.transpose(0, 2, 1, 3).reshape(Bc, Tq, Dm)
        return out @ Wo + bo

    def _L1_ffn_ref(x, Wg, bg, W1, b1, W2, b2):
        import jax, jax.numpy as jnp
        import numpy as np
        D_MODEL = 128
        NUM_EXPERTS = 8
        TOP_K = 2
        B, S = (4, 256)
        Bb, Ss, D = x.shape
        E = Wg.shape[1]
        xf = x.reshape(-1, D)
        logits = xf @ Wg + bg
        probs = jax.nn.softmax(logits, axis=-1)
        w, idx = jax.lax.top_k(probs, TOP_K)
        w = w / jnp.sum(w, axis=-1, keepdims=True)
        comb = jnp.sum(jax.nn.one_hot(idx, E, dtype=xf.dtype) * w[..., None], axis=1)
        h = jax.nn.relu(jnp.einsum('nd,edh->enh', xf, W1) + b1[:, None, :])
        y = jnp.einsum('enh,ehd->end', h, W2) + b2[:, None, :]
        out = jnp.einsum('end,ne->nd', y, comb)
        return out.reshape(Bb, Ss, D)
    x = x + _L0_xattn_ref(_layernorm(x, axis=-1), ctx_1024, L0_xattn_Wq, L0_xattn_bq, L0_xattn_Wk, L0_xattn_bk, L0_xattn_Wv, L0_xattn_bv, L0_xattn_Wo, L0_xattn_bo, L0_xattn_gamma, L0_xattn_beta)
    x = x + _L0_ffn_ref(_layernorm(x, axis=-1), L0_ffn_wf, L0_ffn_uf, L0_ffn_bf, L0_ffn_wi, L0_ffn_ui, L0_ffn_bi, L0_ffn_wc, L0_ffn_uc, L0_ffn_bc, L0_ffn_wo, L0_ffn_uo, L0_ffn_bo, L0_ffn_in_c)
    x = x + _L1_xattn_ref(_layernorm(x, axis=-1), ctx_1024, mask_BxS2_bk0, L1_xattn_Wq, L1_xattn_bq, L1_xattn_Wkv, L1_xattn_bkv, L1_xattn_Wo, L1_xattn_bo)
    x = x + _L1_ffn_ref(_layernorm(x, axis=-1), L1_ffn_Wg, L1_ffn_bg, L1_ffn_W1, L1_ffn_b1, L1_ffn_W2, L1_ffn_b2)
    return x

_drawn_inputs = setup_inputs


def setup_inputs(seed=0):
    import zlib

    import numpy as np

    out = dict(_drawn_inputs(seed))
    spreads = {'L0_xattn_gamma': (1.0, 0.2),
     'L0_xattn_beta': (0.0, 0.1),
     'L0_ffn_bf': (0.0, 0.8),
     'L0_ffn_bi': (0.0, 0.326),
     'L0_ffn_bc': (0.0, 0.1),
     'L0_ffn_bo': (0.0, 0.1),
     'L0_ffn_in_c': (0.0, 0.1),
     'L1_ffn_bg': (0.0, 0.1),
     'L1_ffn_b1': (0.0, 0.1),
     'L1_ffn_b2': (0.0, 0.1)}
    factors = {'L0_xattn_bo': 186.765,
     'L1_xattn_Wq': 59.856,
     'L1_xattn_bq': 200.0,
     'L1_xattn_bkv': 6.443,
     'L0_ffn_uf': 2.907}
    for name, (base, spread) in spreads.items():
        noise = np.random.default_rng([zlib.crc32(name.encode()), seed]).standard_normal(out[name].shape)
        drawn = base * np.exp(spread * noise) if base else spread * noise
        out[name] = jnp.asarray(drawn.astype(out[name].dtype))
    for name, factor in factors.items():
        out[name] = (out[name] * factor).astype(out[name].dtype)
    return out
```

```python
from contextlib import ExitStack

import concourse.bass as bass
from concourse import mybir

P = 128
NB = 2
NJ = 4
T = NJ * P
TK = 154
KB = 32
TKP = P + KB
KR = TK - P
H = 16
HD = P // H
HG = 4
HQ = H // HG
GW = 32
HQA = GW // (HD + 1)
HALVES = ((0, 9), (9, 7))
E = 8
HC = 2
BP = 64
EPS_LN = 1e-5
EPS_DEN = 1e-6
MASKED = -3e38
QK_SCALE = float(HD) ** -0.5
SLOTS = ((0, 0), (0, 1), (1, 0), (1, 1), (0, 2), (2, 0))
ROW_MASK = len(SLOTS) * HD
ROW_MAX = ROW_MASK + 1
ROWS_SCORE = ROW_MASK + 1
ROWS_ALL = ROW_MAX + 3

F32 = mybir.dt.float32
F32R = mybir.dt.float32r
BF16 = mybir.dt.bfloat16
U8 = mybir.dt.uint8
U32 = mybir.dt.uint32
ALU = mybir.AluOpType
ACT = mybir.ActivationFunctionType
AX = mybir.AxisListType

W_CTX = ("k0", "v0", "v1", "k1")
W_FFN = ("wf", "wi", "wc", "uf", "ui", "uc", "wo", "uo")
C_BQ0, C_BF, C_BI, C_BC, C_INC, C_BOF, C_BK1, C_BQ1, C_B1 = 0, 1, 2, 3, 4, 5, 6, 7, 8
N_COLS = C_B1 + E * HC
R_BO0, R_GAMMA, R_BETA, R_BO1, R_BG = 0, P, 2 * P, 3 * P, 4 * P
R_BK0, R_BV0, R_BV1 = R_BG + E, R_BG + E + P, R_BG + E + 2 * P
N_ROWS = R_BV1 + P

LN_X, LN_R, LN_X1, LN_X2, LN_X3 = range(5)
N_LN = 5
T_OUT, T_NORM, T_PROJ, T_IN, T_GATE, T_COMB = range(6)
TAIL_UNITS = (3, 6, 9, 13, 16)
TAIL_PE = {0: T_OUT, 1: T_NORM, 2: T_PROJ, 4: T_IN, 5: T_GATE, 7: T_COMB}
TAIL_ACT = {1: T_PROJ, 4: T_IN, 5: T_GATE, 7: T_COMB}
TAIL_DVE = {0: T_NORM, 2: T_PROJ, 3: T_IN, 5: T_GATE}
TAIL_LN = 3


def two_blocks(nc, x, ctxt, mask, w_ctx, w_l0, w_ffn, w_l1, cols, rows, w1, w2, b2, out):
    with ExitStack() as ctx:
        def sb(name, shape, dt=F32):
            return ctx.enter_context(nc.sbuf_tensor(name, shape, dt))

        bank = [ctx.enter_context(nc.psum_tensor(f"bank{i}", [P, 512], F32)) for i in range(8)]

        def sem(name):
            return ctx.enter_context(nc.semaphore(name))

        x_t = sb("x_t", [P, NB, NJ, P])
        ctx_t = sb("ctx_t", [P, NB, TKP])
        ctx_rep = sb("ctx_rep", [P, NB, HG, KB])
        mask_u = sb("mask_u", [1, NB, TKP], U8)
        mask_b = sb("mask_b", [1, NB, TKP], BF16)
        wc_s = sb("wc_s", [P, 4 * P])
        w0_s = sb("w0_s", [P, 2 * P])
        wf_s = sb("wf_s", [P, 8 * P])
        w3_s = sb("w3_s", [P, 2 * P + E])
        col = sb("col", [P, N_COLS])
        row = sb("row", [P, N_ROWS])
        w1_s = sb("w1_s", [P, E, HC * P])
        w2_s = w1_s[:].rearrange("p e (c d) -> p e c d", c=HC)
        w1_h = sb("w1_h", [P, E, HC * P], F32R)
        w1_l = sb("w1_l", [P, E, HC * P], F32R)
        w2_h = sb("w2_h", [P, E, HC, P], F32R)
        w2_l = sb("w2_l", [P, E, HC, P], F32R)
        b2_s = sb("b2_s", [3 * E, P])
        b2_r = sb("b2_r", [3 * E, P])
        b2_part = sb("b2_part", [3 * E, 3, P], BF16)
        pick_e = sb("pick_e", [3 * E, E, P], BF16)
        ident = sb("ident", [P, P])
        ident_b = sb("ident_b", [P, P], BF16)
        ones_b = sb("ones_b", [3, T], BF16)
        m_half = sb("m_half", [P, NJ])
        iota_u = sb("iota_u", [P, E], U32)
        iota_f = sb("iota_f", [P, E])
        bq0_1 = sb("bq0_1", [P, 1])
        bq0_neg = sb("bq0_neg", [P, 1])
        gate0 = sb("gate0", [P, 3])
        gate1 = sb("gate1", [P, 3])
        c0_half = sb("c0_half", [P, 1])
        eps_den = sb("eps_den", [P, 1])
        v_done = sb("v_done", [1, 1])
        stats = sb("stats", [P, N_LN, NB, NJ, 6])
        mv = sb("mv", [P, N_LN, NB, NJ, 2])
        vare = sb("vare", [P, N_LN, NB, NJ])
        rstd = sb("rstd", [P, N_LN, NB, NJ])
        k0 = sb("k0", [P, NB, 2, P])
        k0_b = sb("k0_b", [P, NB, 2, P])
        k0_m = sb("k0_m", [P, NB, 2, P])
        k0_e = sb("k0_e", [P, NB, 2, P])
        v0 = sb("v0", [P, NB, 2, P + 1])
        kv0 = sb("kv0", [P, NB, P + 1])
        a_n = sb("a_n", [P, NB, NJ, P])
        a_bo = sb("a_bo", [P, NB, NJ, P])
        x_beta = sb("x_beta", [P, NB, NJ, P])
        a_f = sb("a_f", [P, NB, T])
        q_m = sb("q_m", [P, NB, T])
        q_e = sb("q_e", [P, NB, T])
        q0 = sb("q0", [P, NB, T])
        den = q_e
        rden = q_m
        u_f = a_f
        r_t = sb("r_t", [P, NB, NJ, P])
        y_t = a_bo
        x1 = sb("x1", [P, NB, NJ, P])
        z_n = a_n
        z_f = q0
        g_act = sb("g_act", [P, NB, 3, T])
        g_f = q_m
        g_i = q_e
        cell = a_bo[:].rearrange("p b j d -> p b (j d)")
        uo_half = sb("uo_half", [P, P])
        h_f = cell
        x2 = x_t
        x2_bo = x_beta
        s_n = a_n
        s_f = a_f
        q1 = q_m
        q_r1 = q_e
        q_part = sb("q_part", [P, NB, 3, T], BF16)
        q_stack = sb("q_stack", [P, H, T], BF16)
        k1 = sb("k1", [P, NB, TKP])
        k_r1 = sb("k_r1", [P, NB, TKP])
        
        k_part = sb("k_part", [P, NB, 3, TKP], BF16)
        k_stack = sb("k_stack", [P, H, TKP], BF16)
        v1 = k0_m
        v_a = sb("v_a", [P, NB, H, GW])
        v_b = sb("v_b", [P, NB, HQ, HG * GW])
        nmax = sb("nmax", [P, NB, NJ, H])
        nm_r1 = sb("nm_r1", [P, NB, NJ, H])
        
        nm_part = [sb(f"nm_part{k}", [P, NB, NJ, 3, n], BF16) for k, (_, n) in enumerate(HALVES)]
        nm_f = [sb(f"nm_f{k}", [3 * n, T], BF16) for k, (_, n) in enumerate(HALVES)]
        o_ev = (q_m, q_e)
        NPR = NB * 3
        prob = g_act[:].rearrange("p s g t -> p (s g) t")
        rsum = sb("rsum", [P, NB, NJ, H])
        o_t = z_n
        o_f = z_f
        x3 = r_t
        e_n = z_n
        e_f = z_f
        e_h = sb("e_h", [P, NB, T], F32R)
        e_l = sb("e_l", [P, NB, T], F32R)
        logit = sb("logit", [P, NB, NJ, E])
        top_v = sb("top_v", [P, NB, NJ, E])
        top_i = sb("top_i", [P, NB, NJ, E], U32)
        top_f = sb("top_f", [P, NB, NJ, E])
        gap = sb("gap", [P, NB, NJ])
        gap_e = sb("gap_e", [P, NB, NJ])
        gap_1 = sb("gap_1", [P, NB, NJ])
        w_top = sb("w_top", [P, NB, 2, NJ])
        hit1 = sb("hit1", [P, NB, NJ, E])
        hit2 = sb("hit2", [P, NB, NJ, E])
        hit1w = sb("hit1w", [P, NB, NJ, E])
        hit2w = sb("hit2w", [P, NB, NJ, E])
        comb = sb("comb", [P, NB, NJ, E])
        comb_r = sb("comb_r", [P, NB, NJ, E])
        comb_part = sb("comb_part", [P, NB, NJ, 3, E], BF16)
        comb_f = sb("comb_f", [3 * E, NB, T], BF16)
        NCB = 3
        comb_b = w1_s[:].rearrange("p e h -> p (e h)")[:, 0:NCB * T].rearrange("p (n t) -> p n t", t=T)
        NH = NPR
        hid = prob
        hid_h = sb("hid_h", [P, NH, T], F32R)
        hid_l = sb("hid_l", [P, NH, T], F32R)
        y_f = q_m
        res = x1

        ld_x = [sem(f"ld_x{b}") for b in range(NB)]
        ld_ctx = sem("ld_ctx")
        ld_row = sem("ld_row")
        ld_col = sem("ld_col")
        ld_mask = sem("ld_mask")
        ld_b2 = sem("ld_b2")
        ld_w0 = sem("ld_w0")
        ld_wf = sem("ld_wf")
        ld_w3 = sem("ld_w3")
        ld_w1 = sem("ld_w1")
        ld_w2 = sem("ld_w2")
        pool_step = sem("pool_step")
        consts_ready = sem("consts_ready")
        dve_step = sem("dve_step")
        eps_ready = sem("eps_ready")
        bq0_ready = sem("bq0_ready")
        v_pad = sem("v_pad")
        v_ready = sem("v_ready")
        k1_ready = sem("k1_ready")
        den_ready = sem("den_ready")
        b2_ready = sem("b2_ready")
        pad_ready = sem("pad_ready")
        mask_ready = sem("mask_ready")
        ctx_rep_ready = sem("ctx_rep_ready")
        var_ready = sem("var_ready")
        rstd_ready = sem("rstd_ready")
        ctx_a_mm = sem("ctx_a_mm")
        ctx_b_mm = sem("ctx_b_mm")
        k1_mm = sem("k1_mm")
        k0_neg = sem("k0_neg")
        k0_exp = sem("k0_exp")
        k0_ready = sem("k0_ready")
        v0_ready = sem("v0_ready")
        v1_ready = sem("v1_ready")
        kv0_mm = sem("kv0_mm")
        kv0_ready = sem("kv0_ready")
        gate_c_mm = sem("gate_c_mm")
        gate_c_ready = sem("gate_c_ready")
        k_parts = sem("k_parts")
        k_stacked = [sem(f"k_stacked{b}") for b in range(NB)]
        a_ready = sem("a_ready")
        a_tr = sem("a_tr")
        a_f_ready = sem("a_f_ready")
        a_bo_ready = sem("a_bo_ready")
        q0_mm = sem("q0_mm")
        q0_neg = sem("q0_neg")
        q0_exp = sem("q0_exp")
        q0_ready = sem("q0_ready")
        num_mm = sem("num_mm")
        u_ready = sem("u_ready")
        att0_mm = sem("att0_mm")
        x_beta_ready = sem("x_beta_ready")
        z_ready = sem("z_ready")
        z_tr = sem("z_tr")
        z_f_ready = sem("z_f_ready")
        gates_mm = sem("gates_mm")
        gates_act = sem("gates_act")
        cell_ready = sem("cell_ready")
        uo_ready = sem("uo_ready")
        h_mm = sem("h_mm")
        h_act = sem("h_act")
        h_tr = sem("h_tr")
        x2_ready = sem("x2_ready")
        s_ready = sem("s_ready")
        s_tr = sem("s_tr")
        s_f_ready = sem("s_f_ready")
        q1_mm = sem("q1_mm")
        q_parts = sem("q_parts")
        q_stacked = [sem(f"q_stacked{b}") for b in range(NB)]
        score_mm = sem("score_mm")
        max_taken = sem("max_taken")
        nm_parts = sem("nm_parts")
        nm_tr = sem("nm_tr")
        nm_f_ready = sem("nm_f_ready")
        nm_stacked = [[sem(f"nm_stacked{b}_{k}") for k in range(2)] for b in range(NB)]
        st_mm = sem("st_mm")
        prob_ready = sem("prob_ready")
        pv_mm = sem("pv_mm")
        o_ev_ready = sem("o_ev_ready")
        o_turned = sem("o_turned")
        o_ready = sem("o_ready")
        o_tr = sem("o_tr")
        o_f_ready = sem("o_f_ready")
        att1_mm = sem("att1_mm")
        x2_bo_ready = sem("x2_bo_ready")
        x3_ready = sem("x3_ready")
        w_hi = sem("w_hi")
        w_lo = sem("w_lo")
        e_ready = sem("e_ready")
        e_tr = sem("e_tr")
        e_f_ready = sem("e_f_ready")
        e_h_ready = sem("e_h_ready")
        e_l_ready = sem("e_l_ready")
        logit_mm = sem("logit_mm")
        gap_ready = sem("gap_ready")
        gap_exp = sem("gap_exp")
        comb_ready = sem("comb_ready")
        comb_tr = sem("comb_tr")
        comb_f_ready = sem("comb_f_ready")
        comb_b_mm = sem("comb_b_mm")
        comb_b_ready = sem("comb_b_ready")
        h1_mm = sem("h1_mm")
        hid_full = sem("hid_full")
        weighted = sem("weighted")
        hid_hi = [sem(f"hid_hi{c}") for c in range(HC)]
        hid_lo_pool = sem("hid_lo_pool")
        hid_lo_dve = sem("hid_lo_dve")
        y_mm = sem("y_mm")
        y_f_ready = sem("y_f_ready")
        y_tr = sem("y_tr")
        res_ready = sem("res_ready")
        stored = sem("stored")

        UPB = H + HQ
        UNITS = [(hq, i) for hq in range(HQ) for i in range(HG + 1)]
        RING = (0, 1, 6, 7)
        PAIR = ((4, 5), (2, 3))
        MAX_GROUPS = [[(g, min(3, h0 + n - g)) for g in range(h0, h0 + n, 3)] for h0, n in HALVES]
        NG = NJ * sum(len(m) for m in MAX_GROUPS)

        def head_col(hq):
            return (HD + 1) * (hq % HQA)

        def lo_on_pool(e, c):
            return c == 0 or e % 2 == 0

        def lo_counts(n):
            at = [lo_on_pool(v // HC % E, v % HC) for v in range(n)]
            return sum(at), n - sum(at)

        block = ctx.enter_context(nc.Block())

        @block.sync
        def _(sp):
            for b in range(NB):
                sp.dma_start(x_t[:, b], x[b].rearrange("(p j) d -> p j d", j=NJ)).then_inc(ld_x[b], 16)
            sp.dma_start(row[:], rows.partition_broadcast(P)).then_inc(ld_row, 16)
            sp.dma_start(w0_s[:], w_l0).then_inc(ld_w0, 16)
            sp.dma_start(wf_s[:], w_ffn).then_inc(ld_wf, 16)
            sp.dma_start(w3_s[:], w_l1).then_inc(ld_w3, 16)
            for p in range(3):
                sp.dma_start(b2_s[p * E:(p + 1) * E], b2).then_inc(ld_b2, 16)
            sp.dma_start(w1_s[:], w1.rearrange("e d h -> d e h")).then_inc(ld_w1, 16)
            sp.wait_ge(mask_ready, 1)
            for b in range(NB):
                sp.dma_start(q_stack[BP * b + ROW_MASK:BP * b + ROW_MASK + 1],
                             ones_b[0:1, :].rearrange("p (o t) -> p o t", o=1).broadcast_to([1, H, T]))\
                  .then_inc(q_stacked[b], 16)
                sp.dma_start(k_stack[BP * b + ROW_MAX:BP * b + ROW_MAX + 3],
                             ones_b[:, 0:TKP].rearrange("p (o t) -> p o t", o=1).broadcast_to([3, H, TKP]))\
                  .then_inc(k_stacked[b], 16)
            sp.wait_ge(k_parts, 1)
            for b in range(NB):
                for s, (_, kp) in enumerate(SLOTS):
                    sp.dma_start(k_stack[BP * b + HD * s:BP * b + HD * s + HD], k_part[:, b, kp])\
                      .then_inc(k_stacked[b], 16)
                sp.dma_start(k_stack[BP * b + ROW_MASK:BP * b + ROW_MASK + 1],
                             mask_b[0:1, b:b + 1, :].broadcast_to([1, H, TKP])).then_inc(k_stacked[b], 16)
            for b in range(NB):
                for part in range(3):
                    sp.wait_ge(q_parts, 3 * b + part + 1)
                    for s, (qp, _) in enumerate(SLOTS):
                        if qp == part:
                            sp.dma_start(q_stack[BP * b + HD * s:BP * b + HD * s + HD], q_part[:, b, qp])\
                              .then_inc(q_stacked[b], 16)
            for b in range(NB):
                for k, (h0, n) in enumerate(HALVES):
                    sp.wait_ge(nm_f_ready, 2 * b + k + 1)
                    sp.dma_start(q_stack[BP * b + ROW_MAX:BP * b + ROW_MAX + 3, h0:h0 + n], nm_f[k][:])\
                      .then_inc(nm_stacked[b][k], 16)
            for b in range(NB):
                sp.wait_ge(res_ready, b + 1)
                sp.dma_start(out[b].rearrange("(p j) d -> p j d", j=NJ), res[:, b]).then_inc(stored, 16)
            sp.wait_ge(stored, 16 * NB)

        @block.gpsimd
        def _(pool):
            steps = [0]

            def link(ins):
                steps[0] += 1
                ins.then_inc(pool_step, 1)
                pool.wait_ge(pool_step, steps[0])

            link(pool.memset(ident[:], 0.0))
            link(pool.affine_select(out=ident[:], in_=ident[:], compare_op=ALU.not_equal, fill=1.0,
                                    base=0, pattern=[[-1, P]], channel_multiplier=1))
            pool.memset(m_half[:], -0.5).then_inc(consts_ready, 1)
            pool.tensor_copy(ident_b[:], ident[:]).then_inc(consts_ready, 1)
            pool.iota(iota_u[:], pattern=[[1, E]], base=0, channel_multiplier=0).then_inc(consts_ready, 1)
            pool.wait_ge(consts_ready, 3)

            def rstd_of(n, b):
                k = n * NB + b
                pool.wait_ge(var_ready, k + 1)
                pool.tensor_tensor(rstd[:, n, b], vare[:, n, b], m_half[:], ALU.pow).then_inc(rstd_ready, 1)

            def weight_lo(k):
                pool.wait_ge(w_hi, k + 1)
                w, h, lo = (w1_s, w1_h, w1_l) if k < 4 else (w2_s, w2_h, w2_l)
                s = slice(2 * (k % 4), 2 * (k % 4) + 2)
                pool.tensor_tensor(lo[:, s], w[:, s], h[:, s].bitcast(F32), ALU.subtract).then_inc(w_lo, 1)

            def add_rows(dst, src, off, b, done):
                v = row[:, off:off + P].rearrange("p (o d) -> p o d", o=1).broadcast_to([P, NJ, P])
                pool.tensor_tensor(dst[:, b], src[:, b], v, ALU.add).then_inc(done, 1)

            for b in range(NB):
                rstd_of(LN_X, b)
            pool.wait_ge(ld_row, 16)
            for b in range(NB):
                pool.wait_ge(a_ready, b + 1)
                add_rows(a_bo, a_n, R_BO0, b, a_bo_ready)
            for b in range(NB):
                pool.wait_ge(ld_x[b], 16)
                add_rows(x_beta, x_t, R_BETA, b, x_beta_ready)
            pool.wait_ge(k1_ready, 1)
            link(pool.tensor_copy(k_part[:, :, 0], k1[:]))
            link(pool.tensor_tensor(k_r1[:], k1[:], k_part[:, :, 0], ALU.subtract))
            link(pool.tensor_copy(k_part[:, :, 1], k_r1[:]))
            pool.tensor_tensor(k_part[:, :, 2], k_r1[:], k_part[:, :, 1], ALU.subtract).then_inc(k_parts, 1)
            for b in range(NB):
                rstd_of(LN_R, b)
            for b in range(NB):
                rstd_of(LN_X1, b)
            pool.wait_ge(v_pad, 1)
            for b in range(NB):
                pool.wait_ge(v1_ready, b + 1)
                for hq in range(HQ):
                    c0 = head_col(hq)
                    s = slice(hq * HG * HD, (hq + 1) * HG * HD)
                    link(pool.tensor_tensor(v_a[:, b, hq * HG:(hq + 1) * HG, c0:c0 + HD],
                                            v1[:, b, 0, s].rearrange("p (g d) -> p g d", d=HD),
                                            row[:, R_BV1 + s.start:R_BV1 + s.stop].rearrange("p (g d) -> p g d", d=HD),
                                            ALU.add))
                    for g in range(HG):
                        q = slice(KB * g, KB * g + KB)
                        f = slice((hq * HG + g) * HD, (hq * HG + g + 1) * HD)
                        link(pool.tensor_tensor(v_b[q, b, hq, GW * g + c0:GW * g + c0 + HD], v1[q, b, 1, f],
                                                row[q, R_BV1 + f.start:R_BV1 + f.stop], ALU.add))
            pool.memset(v_done[:], 0.0).then_inc(v_ready, 1)
            for k in range(0, 4):
                weight_lo(k)
            pool.wait_ge(w_lo, 4)
            pool.dma_start(w2_s[:], w2.rearrange("e (c p) d -> p e c d", p=P)).then_inc(ld_w2, 16)
            for b in range(NB):
                rstd_of(LN_X2, b)
            for b in range(NB):
                add_rows(x2_bo, x2, R_BO1, b, x2_bo_ready)
            def rows_of(k):
                return ident[0:3 * E, k * E:(k + 1) * E].rearrange("p (e o) -> p e o", o=1)\
                    .broadcast_to([3 * E, E, P])
            link(pool.tensor_tensor(pick_e[:], rows_of(0), rows_of(1), ALU.add))
            link(pool.tensor_tensor(pick_e[:], pick_e[:], rows_of(2), ALU.add))
            pool.wait_ge(ld_b2, 48)
            link(pool.tensor_copy(b2_part[:, 0], b2_s[:]))
            link(pool.tensor_tensor(b2_r[:], b2_s[:], b2_part[:, 0], ALU.subtract))
            link(pool.tensor_copy(b2_part[:, 1], b2_r[:]))
            pool.tensor_tensor(b2_part[:, 2], b2_r[:], b2_part[:, 1], ALU.subtract).then_inc(b2_ready, 1)
            for k in range(4, 8):
                weight_lo(k)

            def hidden_lo(b, e):
                for c in range(HC):
                    if not lo_on_pool(e, c):
                        continue
                    g = (b * E + e) * HC + c
                    pool.wait_ge(hid_hi[c], b * E + e + 1)
                    if g >= NH:
                        pool.wait_ge(y_mm, (g - NH) // HC + 1)
                    pool.tensor_tensor(hid_l[:, g % NH], hid[:, g % NH], hid_h[:, g % NH].bitcast(F32),
                                       ALU.subtract).then_inc(hid_lo_pool, 1)

            rstd_of(LN_X3, 0)
            for e in range(E):
                if e == TAIL_LN:
                    rstd_of(LN_X3, 1)
                hidden_lo(0, e)
            for e in range(E):
                hidden_lo(1, e)

        @block.scalar
        def _(act):
            act.dma_start(ctx_t[:, :, 0:TK], ctxt).then_inc(ld_ctx, 16)
            act.dma_start(wc_s[:], w_ctx).then_inc(ld_ctx, 16)
            act.dma_start(col[:], cols).then_inc(ld_col, 16)
            act.dma_start(mask_u[:, :, 0:TK], mask).then_inc(ld_mask, 16)

            def copy_out(src, dst, ready, n, done):
                act.wait_ge(ready, n)
                nc.scalar.activation(dst, src, ACT.Copy).then_inc(done, 1)

            def weight_hi(k):
                act.wait_ge(ld_w1 if k < 4 else ld_w2, 16)
                w, h = (w1_s, w1_h) if k < 4 else (w2_s, w2_h)
                s = slice(2 * (k % 4), 2 * (k % 4) + 2)
                nc.scalar.activation(h[:, s], w[:, s], ACT.Copy).then_inc(w_hi, 1)

            def values_out(b):
                act.wait_ge(v0_ready, b + 1)
                nc.scalar.activation(v1[:, b, 0], bank[b][:, 2 * P:3 * P], ACT.Copy)
                nc.scalar.activation(v1[:, b, 1], bank[2 + b][:, 2 * P:3 * P], ACT.Copy).then_inc(v1_ready, 1)

            for b in range(NB):
                act.wait_ge(k0_neg, b + 1)
                nc.scalar.activation(k0_e[:, b], k0_m[:, b], ACT.Exp).then_inc(k0_exp, 1)
                copy_out(bank[6 + b][:], a_f[:, b], a_tr, b + 1, a_f_ready)
                act.wait_ge(q0_mm, b + 1)
                if b == 0:
                    act.wait_ge(bq0_ready, 1)
                nc.scalar.activation(q_m[:, b], bank[6 + b][:], ACT.Relu, bias=bq0_neg[:], scale=-1.0)\
                  .then_inc(q0_neg, 1)
                act.wait_ge(q0_neg, b + 1)
                nc.scalar.activation(q_e[:, b], q_m[:, b], ACT.Exp, scale=-1.0).then_inc(q0_exp, 1)
            act.wait_ge(k1_mm, 1)
            act.wait_ge(ld_col, 16)
            nc.scalar.activation(k1[:], bank[4][:, 0:NB * TKP].rearrange("p (b k) -> p b k", b=NB), ACT.Identity,
                                 bias=col[:, C_BK1:C_BK1 + 1], scale=1.0).then_inc(k1_ready, 1)
            act.wait_ge(kv0_ready, 1)
            for b in range(NB):
                act.wait_ge(q0_ready, b + 1)
                nc.scalar.activation(den[:, b], q0[:, b], ACT.Identity, bias=eps_den[:],
                                     scale=kv0[:, b, P:P + 1]).then_inc(den_ready, 1)
            for b in range(NB):
                values_out(b)
            act.wait_ge(ld_wf, 16)
            nc.scalar.activation(uo_half[:], wf_s[:, 7 * P:8 * P], ACT.Copy, scale=0.5).then_inc(uo_ready, 1)
            for k in range(4):
                weight_hi(k)
            for b in range(NB):
                copy_out(bank[6 + b][:], z_f[:, b], z_tr, b + 1, z_f_ready)
            for step in range(NB):
                bias = gate0 if step == 0 else gate1
                for g in range(3):
                    act.wait_ge(gates_mm, 3 * step + g + 1)
                    nc.scalar.activation(g_act[:, step, g], bank[3 * step + g][:], ACT.Tanh,
                                         bias=bias[:, g:g + 1], scale=1.0 if g == 2 else 0.5).then_inc(gates_act, 1)
            for b in range(NB):
                act.wait_ge(h_mm, b + 1)
                nc.scalar.activation(h_f[:, b], bank[b][:], ACT.Tanh, bias=col[:, C_BOF:C_BOF + 1],
                                     scale=1.0).then_inc(h_act, 1)
            for b in range(NB):
                copy_out(bank[2 + b][:], s_f[:, b], s_tr, b + 1, s_f_ready)
            for k in range(4, 8):
                weight_hi(k)

            def max_out(b, k):
                n = 3 * HALVES[k][1]
                if b == 1:
                    act.wait_ge(nm_stacked[0][k], 16)
                copy_out(bank[2 + k][0:n, 0:T // 2].bitcast(BF16), nm_f[k][:], nm_tr, 2 * b + k + 1, nm_f_ready)

            def exps(b, n):
                u = b * UPB + n
                act.wait_ge(st_mm, u + 1)
                if u >= NPR:
                    act.wait_ge(pv_mm, u - NPR + 1)
                nc.scalar.activation(prob[:, u % NPR], bank[RING[u % 4]][:], ACT.Exp).then_inc(prob_ready, 1)

            def tail(b, piece):
                first, second = (bank[i][:] for i in PAIR[b])
                if piece == T_OUT:
                    act.wait_ge(pv_mm, (b + 1) * UPB)
                    nc.scalar.activation(o_ev[0][:, b], first, ACT.Copy)
                    nc.scalar.activation(o_ev[1][:, b], second, ACT.Copy).then_inc(o_ev_ready, 1)
                elif piece == T_PROJ:
                    copy_out(first, o_f[:, b], o_tr, b + 1, o_f_ready)
                elif piece == T_IN:
                    copy_out(first, e_h[:, b], e_tr, b + 1, e_h_ready)
                    nc.scalar.activation(e_f[:, b], first, ACT.Copy).then_inc(e_f_ready, 1)
                elif piece == T_GATE:
                    act.wait_ge(gap_ready, b + 1)
                    nc.scalar.activation(gap_e[:, b], gap[:, b], ACT.Exp).then_inc(gap_exp, 1)
                elif piece == T_COMB:
                    copy_out(bank[PAIR[b][0]][0:3 * E, 0:T // 2].bitcast(BF16), comb_f[:, b], comb_tr, b + 1,
                             comb_f_ready)

            def spread_comb(n):
                b = n // E
                act.wait_ge(comb_b_mm, n + 1)
                if n >= NCB:
                    act.wait_ge(weighted, (n - NCB + 1) * HC)
                nc.scalar.activation(comb_b[:, n % NCB], bank[PAIR[b][1]][:], ACT.Copy).then_inc(comb_b_ready, 1)

            def hidden(n):
                b, e = divmod(n, E)
                for c in range(HC):
                    g = n * HC + c
                    act.wait_ge(h1_mm, g + 1)
                    if g >= NH:
                        act.wait_ge(y_mm, (g - NH) // HC + 1)
                        n_pool, n_dve = lo_counts(g - NH + 1)
                        act.wait_ge(hid_lo_pool, n_pool)
                        if n_dve:
                            act.wait_ge(hid_lo_dve, n_dve)
                    v = e * HC + c
                    nc.scalar.activation(hid[:, g % NH], bank[RING[g % 4]][:], ACT.Relu,
                                         bias=col[:, C_B1 + v:C_B1 + v + 1], scale=1.0).then_inc(hid_full, 1)

            def hidden_hi(n):
                g = n * HC + 1
                act.wait_ge(weighted, g + 1)
                nc.scalar.activation(hid_h[:, g % NH], hid[:, g % NH], ACT.Copy).then_inc(hid_hi[1], 1)

            for k in range(2):
                max_out(0, k)
            for n in range(UPB):
                exps(0, n)
            for k in range(2):
                max_out(1, k)
            for n in range(UPB):
                if n in TAIL_UNITS:
                    tail(0, TAIL_UNITS.index(n))
                exps(1, n)
            tail(0, T_COMB)
            tail(1, T_OUT)
            for n in range(NB * E + 1):
                if n < NB * E:
                    spread_comb(n)
                    hidden(n)
                    if n in TAIL_ACT:
                        tail(1, TAIL_ACT[n])
                if n >= 1:
                    hidden_hi(n - 1)
                if n >= 1 and n % E == 2 and n > E:
                    copy_out(bank[PAIR[0][0]][:], y_f[:, 0], y_mm, E, y_f_ready)
            copy_out(bank[PAIR[1][0]][:], y_f[:, 1], y_mm, NB * E, y_f_ready)

        @block.tensor
        def _(pe):
            def transposes(dst, src, done):
                for j in range(NJ):
                    last = pe.transpose(dst[:, j * P:(j + 1) * P], src[:, j], ident[:])
                last.then_inc(done, 1)

            pe.wait_ge(ld_ctx, 32)
            pe.wait_ge(pad_ready, 1)
            for b in range(NB):
                pe.matmul(bank[b][:, 0:3 * P], ctx_t[:, b, 0:P], wc_s[:, 0:3 * P], start=True, stop=True)\
                  .then_inc(ctx_a_mm, 1)
                if b == 0:
                    pe.wait_ge(ctx_rep_ready, 1)
                pe.matmul(bank[2 + b][:, 0:3 * P], ctx_rep[:, b], wc_s[:, 0:3 * P], start=True, stop=True)\
                  .then_inc(ctx_b_mm, 1)
                if b == 0:
                    pe.wait_ge(consts_ready, 3)
                pe.wait_ge(a_ready, b + 1)
                transposes(bank[6 + b], a_n[:, b], a_tr)
                pe.wait_ge(ld_w0, 16)
                pe.wait_ge(a_f_ready, b + 1)
                pe.matmul(bank[6 + b][:], w0_s[:, 0:P], a_f[:, b], start=True, stop=True).then_inc(q0_mm, 1)
            pe.matmul(bank[4][:, 0:NB * TKP], wc_s[:, 3 * P:4 * P], ctx_t[:], start=True, stop=True)\
              .then_inc(k1_mm, 1)
            for b in range(NB):
                pe.wait_ge(k0_ready, b + 1)
                pe.wait_ge(v0_ready, b + 1)
                o = bank[5][:, 256 * b:256 * b + P + 1]
                pe.matmul(o, k0[:, b, 0], v0[:, b, 0], start=True, stop=False)
                pe.matmul(o, k0[0:KR, b, 1], v0[0:KR, b, 1], start=False, stop=True).then_inc(kv0_mm, 1)
            pe.wait_ge(kv0_ready, 1)
            pe.wait_ge(ld_wf, 16)
            pe.wait_ge(ld_col, 16)
            for g in range(3):
                last = pe.matmul(bank[5][:, g:g + 1], wf_s[:, (3 + g) * P:(4 + g) * P], col[:, C_INC:C_INC + 1],
                                 start=True, stop=True)
            last.then_inc(gate_c_mm, 1)
            for b in range(NB):
                pe.wait_ge(q0_ready, b + 1)
                pe.matmul(bank[6 + b][:], kv0[:, b, 0:P], q0[:, b], start=True, stop=True).then_inc(num_mm, 1)
            pe.wait_ge(gate_c_ready, 1)
            pe.wait_ge(k1_ready, 1)
            for b in range(NB):
                pe.wait_ge(u_ready, b + 1)
                for j in range(NJ):
                    last = pe.matmul(bank[4 + b][:, j * P:(j + 1) * P], u_f[:, b, j * P:(j + 1) * P],
                                     w0_s[:, P:2 * P], start=True, stop=True)
                last.then_inc(att0_mm, 1)
            for b in range(NB):
                pe.wait_ge(z_ready, b + 1)
                transposes(bank[6 + b], z_n[:, b], z_tr)
            pe.wait_ge(v1_ready, NB)
            for step in range(NB):
                pe.wait_ge(z_f_ready, step + 1)
                for g in range(3):
                    mm = pe.matmul(bank[3 * step + g][:], wf_s[:, g * P:(g + 1) * P], z_f[:, step],
                                   start=True, stop=step == 0)
                    if step == 0:
                        mm.then_inc(gates_mm, 1)
            for b in range(NB):
                pe.wait_ge(gates_act, b + 1)
                pe.matmul(bank[b][:], wf_s[:, 6 * P:7 * P], z_f[:, b], start=True, stop=False)
            pe.wait_ge(cell_ready, 1)
            for g in range(3):
                pe.matmul(bank[3 + g][:], wf_s[:, (3 + g) * P:(4 + g) * P], cell[:, 0], start=False, stop=True)\
                  .then_inc(gates_mm, 1)
            pe.wait_ge(uo_ready, 1)
            pe.wait_ge(cell_ready, 2)
            for b in range(NB):
                pe.matmul(bank[b][:], uo_half[:], cell[:, 1], start=False, stop=True).then_inc(h_mm, 1)
            for b in range(NB):
                pe.wait_ge(h_act, b + 1)
                for j in range(NJ):
                    last = pe.transpose(bank[6 + b][:, j * P:(j + 1) * P], h_f[:, b, j * P:(j + 1) * P], ident[:])
                last.then_inc(h_tr, 1)
            pe.wait_ge(gates_act, 6)
            pe.wait_ge(ld_w3, 16)
            for b in range(NB):
                pe.wait_ge(s_ready, b + 1)
                transposes(bank[2 + b], s_n[:, b], s_tr)
                pe.wait_ge(s_f_ready, b + 1)
                pe.matmul(bank[4 + b][:], w3_s[:, 0:P], s_f[:, b], start=True, stop=True).then_inc(q1_mm, 1)

            def scores(b, ring):
                n = b * NG
                for k, groups in enumerate(MAX_GROUPS):
                    for j in range(NJ):
                        for h0, nh in groups:
                            m = n - b * NG
                            if m >= len(ring):
                                pe.wait_ge(max_taken, n - len(ring) + 1)
                            for i in range(nh):
                                last = pe.matmul(bank[ring[m % len(ring)]][:, i * TK:(i + 1) * TK],
                                                 q_stack[BP * b:BP * b + ROWS_SCORE, h0 + i, j * P:(j + 1) * P],
                                                 k_stack[BP * b:BP * b + ROWS_SCORE, h0 + i, 0:TK],
                                                 start=True, stop=True)
                            last.then_inc(score_mm, 1)
                            n += 1
                            yield None

            def max_turn(b, k):
                pe.wait_ge(nm_parts, 2 * b + k + 1)
                h0, n = HALVES[k]
                nm_ps = bank[2 + k][0:3 * n, 0:T // 2].bitcast(BF16)
                for j in range(NJ):
                    last = pe.transpose(nm_ps[:, j * P:(j + 1) * P], nm_part[k][:, b, j], ident_b[:])
                last.then_inc(nm_tr, 1)

            def st(b, n):
                u = b * UPB + n
                hq, i = UNITS[n]
                pe.wait_ge(nm_stacked[b][0], 16)
                if min(hq * HG + i, H - 1) >= HALVES[1][0] or hq * HG + HG > HALVES[1][0]:
                    pe.wait_ge(nm_stacked[b][1], 16)
                if u < 4:
                    pe.wait_ge(max_taken, NG)
                else:
                    pe.wait_ge(prob_ready, u - 3)
                o = bank[RING[u % 4]]
                if i < HG:
                    last = pe.matmul(o[:], k_stack[BP * b:BP * b + ROWS_ALL, hq * HG + i, 0:P],
                                     q_stack[BP * b:BP * b + ROWS_ALL, hq * HG + i], start=True, stop=True)
                else:
                    for g in range(HG):
                        last = pe.matmul(o[KB * g:KB * g + KB], k_stack[BP * b:BP * b + ROWS_ALL, hq * HG + g, P:TKP],
                                         q_stack[BP * b:BP * b + ROWS_ALL, hq * HG + g], start=True, stop=True)
                last.then_inc(st_mm, 1)

            def pv(b, n):
                u = b * UPB + n
                hq, i = UNITS[n]
                o = bank[PAIR[b][hq // HQA]]
                pe.wait_ge(prob_ready, u + 1)
                if n == 0 and b == 0:
                    pe.wait_ge(v_ready, 1)
                    pe.wait_ge(q_parts, 3 * NB)
                if i < HG:
                    last = pe.matmul(o[GW * i:GW * i + GW], v_a[:, b, hq * HG + i], prob[:, u % NPR],
                                     start=hq % HQA == 0, stop=False, skip_group_check=True)
                else:
                    last = pe.matmul(o[:], v_b[:, b, hq], prob[:, u % NPR], start=False,
                                     stop=hq % HQA == HQA - 1 or hq == HQ - 1, skip_group_check=True)
                last.then_inc(pv_mm, 1)

            LAG = 3

            def attend(b, n):
                if n < UPB:
                    st(b, n)
                if n >= LAG:
                    pv(b, n - LAG)

            def tail(b, piece):
                first, second = (bank[i] for i in PAIR[b])
                if piece == T_OUT:
                    pe.wait_ge(o_ev_ready, b + 1)
                    for k, dst in enumerate((first, second)):
                        for j in range(NJ):
                            last = pe.transpose(dst[:, j * P:(j + 1) * P], o_ev[k][:, b, j * P:(j + 1) * P], ident[:])
                    last.then_inc(o_turned, 1)
                elif piece == T_NORM:
                    pe.wait_ge(o_ready, b + 1)
                    transposes(first, o_t[:, b], o_tr)
                elif piece == T_PROJ:
                    pe.wait_ge(o_f_ready, b + 1)
                    for j in range(NJ):
                        last = pe.matmul(second[:, j * P:(j + 1) * P], o_f[:, b, j * P:(j + 1) * P],
                                         w3_s[:, P:2 * P], start=True, stop=True)
                    last.then_inc(att1_mm, 1)
                elif piece == T_IN:
                    pe.wait_ge(e_ready, b + 1)
                    transposes(first, e_n[:, b], e_tr)
                elif piece == T_GATE:
                    pe.wait_ge(e_f_ready, b + 1)
                    for j in range(NJ):
                        last = pe.matmul(second[:, j * E:(j + 1) * E], e_f[:, b, j * P:(j + 1) * P],
                                         w3_s[:, 2 * P:2 * P + E], start=True, stop=True)
                    last.then_inc(logit_mm, 1)
                elif piece == T_COMB:
                    pe.wait_ge(comb_ready, b + 1)
                    pe.wait_ge(e_l_ready, b + 1)
                    comb_ps = first[0:3 * E, 0:T // 2].bitcast(BF16)
                    for j in range(NJ):
                        last = pe.transpose(comb_ps[:, j * P:(j + 1) * P], comb_part[:, b, j], ident_b[:])
                    last.then_inc(comb_tr, 1)

            def comb_spread(n):
                b, e = divmod(n, E)
                if e == 0:
                    pe.wait_ge(comb_f_ready, b + 1)
                else:
                    pe.wait_ge(comb_b_ready, n)
                pe.matmul(bank[PAIR[b][1]][:], pick_e[:, e], comb_f[:, b], start=True, stop=True)\
                  .then_inc(comb_b_mm, 1)

            def up(n):
                b, e = divmod(n, E)
                if e == 0:
                    pe.wait_ge(e_l_ready, b + 1)
                for c in range(HC):
                    g = n * HC + c
                    if g == 0:
                        pe.wait_ge(prob_ready, NB * UPB)
                    if g >= 4:
                        pe.wait_ge(hid_full, g - 3)
                    o = bank[RING[g % 4]][:]
                    wh, wl = w1_h[:, e, c * P:(c + 1) * P], w1_l[:, e, c * P:(c + 1) * P]
                    pe.matmul(o, wh, e_h[:, b], start=True, stop=False)
                    pe.matmul(o, wh, e_l[:, b], start=False, stop=False)
                    pe.matmul(o, wl, e_h[:, b], start=False, stop=True).then_inc(h1_mm, 1)

            def down(n):
                b, e = divmod(n, E)
                y = bank[PAIR[b][0]][:]
                if e == 0:
                    pe.wait_ge(b2_ready, 1)
                    for k in range(3):
                        pe.matmul(y, b2_part[:, k], comb_f[:, b], start=k == 0, stop=False)
                for c in range(HC):
                    g = n * HC + c
                    pe.wait_ge(hid_hi[c], n + 1)
                    n_pool, n_dve = lo_counts(g + 1)
                    pe.wait_ge(hid_lo_pool, n_pool)
                    if n_dve:
                        pe.wait_ge(hid_lo_dve, n_dve)
                    hh, hl = hid_h[:, g % NH], hid_l[:, g % NH]
                    pe.matmul(y, w2_h[:, e, c], hh, start=False, stop=False)
                    pe.matmul(y, w2_l[:, e, c], hh, start=False, stop=False)
                    last = pe.matmul(y, w2_h[:, e, c], hl, start=False, stop=e == E - 1 and c == HC - 1)
                last.then_inc(y_mm, 1)

            def y_turn(b):
                pe.wait_ge(y_f_ready, b + 1)
                for j in range(NJ):
                    last = pe.transpose(bank[PAIR[b][1]][:, j * P:(j + 1) * P], y_f[:, b, j * P:(j + 1) * P], ident[:])
                last.then_inc(y_tr, 1)

            pe.wait_ge(q_stacked[0], 16 * (len(SLOTS) + 1))
            pe.wait_ge(k_stacked[0], 16 * (len(SLOTS) + 2))
            pe.wait_ge(x2_ready, NB)
            half = NJ * len(MAX_GROUPS[0])
            for m, _ in enumerate(scores(0, RING)):
                if m == half + 3:
                    max_turn(0, 0)
            max_turn(0, 1)
            pe.wait_ge(nm_f_ready, 2)
            pe.wait_ge(q_stacked[1], 16 * (len(SLOTS) + 1))
            pe.wait_ge(k_stacked[1], 16 * (len(SLOTS) + 2))
            other = scores(1, PAIR[1])
            for n in range(UPB + LAG):
                attend(0, n)
                next(other, None)
                if n % 5 == 4:
                    next(other, None)
            for _ in other:
                pass
            pe.wait_ge(max_taken, 2 * NG)
            max_turn(1, 0)
            max_turn(1, 1)
            pe.wait_ge(nm_f_ready, 4)
            for n in range(UPB + LAG):
                attend(1, n)
                if n in TAIL_UNITS:
                    tail(0, TAIL_UNITS.index(n))
            tail(0, T_COMB)
            pe.wait_ge(w_lo, 8)
            comb_spread(0)
            for n in range(NB * E + 2):
                if n < NB * E:
                    up(n)
                if n in TAIL_PE:
                    tail(1, TAIL_PE[n])
                if n >= 2:
                    down(n - 2)
                if n + 1 < NB * E:
                    comb_spread(n + 1)
                if n == E + 3:
                    y_turn(0)
            y_turn(1)

        @block.vector
        def _(dve):
            steps = [0]

            def link(ins):
                steps[0] += 1
                ins.then_inc(dve_step, 1)
                dve.wait_ge(dve_step, steps[0])

            def ln_stats(n, b, src):
                for j in range(NJ):
                    last = dve.bn_stats(stats[:, n, b, j], src[:, b, j])
                link(last)
                for j in range(NJ):
                    last = dve.bn_aggr(mv[:, n, b, j], stats[:, n, b, j])
                link(last)
                dve.tensor_scalar(vare[:, n, b], mv[:, n, b, :, 1], EPS_LN, None, ALU.add).then_inc(var_ready, 1)

            def ln_apply(n, b, src, dst):
                dve.wait_ge(rstd_ready, n * NB + b + 1)
                for j in range(NJ):
                    last = dve.scalar_tensor_tensor(out=dst[:, b, j], in0=src[:, b, j], scalar=mv[:, n, b, j, 0:1],
                                                    in1=rstd[:, n, b, j:j + 1].broadcast_to([P, P]),
                                                    op0=ALU.subtract, op1=ALU.mult)
                return last

            def by_tile(ap):
                return ap.rearrange("p (j d) -> p j d", j=NJ)

            dve.memset(ctx_t[:, :, TK:TKP], 0.0).then_inc(pad_ready, 1)
            dve.memset(eps_den[:], EPS_DEN).then_inc(eps_ready, 1)
            dve.memset(v0[:, :, :, P:P + 1], 1.0)
            link(dve.memset(mask_b[:], MASKED))
            dve.wait_ge(ld_ctx, 32)
            for g in range(HG):
                last = dve.tensor_copy(ctx_rep[:, :, g], ctx_t[:, :, P:TKP])
            last.then_inc(ctx_rep_ready, 1)
            for b in range(NB):
                dve.wait_ge(ld_x[b], 16)
                ln_stats(LN_X, b, x_t)
            dve.wait_ge(ld_col, 16)
            dve.tensor_scalar(bq0_1[:], col[:, C_BQ0:C_BQ0 + 1], 1.0, None, ALU.add)
            dve.tensor_scalar(bq0_neg[:], col[:, C_BQ0:C_BQ0 + 1], -1.0, None, ALU.mult).then_inc(bq0_ready, 1)
            dve.wait_ge(ld_row, 16)
            for b in range(NB):
                ln_apply(LN_X, b, x_t, a_n).then_inc(a_ready, 1)
                dve.wait_ge(ctx_a_mm, b + 1)
                dve.tensor_tensor(k0_b[:, b, 0], bank[b][:, 0:P], row[:, R_BK0:R_BK0 + P], ALU.add)
                dve.wait_ge(ctx_b_mm, b + 1)
                link(dve.tensor_tensor(k0_b[:, b, 1], bank[2 + b][:, 0:P], row[:, R_BK0:R_BK0 + P], ALU.add))
                dve.tensor_scalar(k0_m[:, b], k0_b[:, b], 0.0, None, ALU.min).then_inc(k0_neg, 1)
                dve.tensor_tensor(v0[:, b, 0, 0:P], bank[b][:, P:2 * P], row[:, R_BV0:R_BV0 + P], ALU.add)
                dve.tensor_tensor(v0[:, b, 1, 0:P], bank[2 + b][:, P:2 * P], row[:, R_BV0:R_BV0 + P],
                                  ALU.add).then_inc(v0_ready, 1)
                dve.wait_ge(k0_exp, b + 1)
                dve.scalar_tensor_tensor(out=k0[:, b], in0=k0_b[:, b], scalar=1.0, in1=k0_e[:, b],
                                         op0=ALU.add, op1=ALU.max).then_inc(k0_ready, 1)
            dve.wait_ge(kv0_mm, NB)
            dve.tensor_copy(kv0[:], bank[5][:].rearrange("p (b c) -> p b c", b=NB)[:, :, 0:P + 1])\
               .then_inc(kv0_ready, 1)
            for b in range(NB):
                dve.wait_ge(q0_exp, b + 1)
                dve.scalar_tensor_tensor(out=q0[:, b], in0=bank[6 + b][:], scalar=bq0_1[:], in1=q_e[:, b],
                                         op0=ALU.add, op1=ALU.max).then_inc(q0_ready, 1)
            dve.wait_ge(gate_c_mm, 1)
            dve.tensor_tensor(gate0[:, 2:3], bank[5][:, 2:3], col[:, C_BC:C_BC + 1], ALU.add)
            dve.tensor_scalar(gate0[:, 0:1], bank[5][:, 0:1], col[:, C_BF:C_BF + 1], 0.5, ALU.add, ALU.mult)
            dve.tensor_scalar(gate0[:, 1:2], bank[5][:, 1:2], col[:, C_BI:C_BI + 1], 0.5, ALU.add, ALU.mult)
            dve.tensor_scalar(gate1[:, 0:2], col[:, C_BF:C_BF + 2], 0.5, None, ALU.mult)
            dve.tensor_copy(gate1[:, 2:3], col[:, C_BC:C_BC + 1])
            dve.tensor_scalar(c0_half[:], col[:, C_INC:C_INC + 1], 0.5, None, ALU.mult).then_inc(gate_c_ready, 1)
            for b in range(NB):
                dve.wait_ge(den_ready, b + 1)
                link(dve.reciprocal(rden[:, b], den[:, b]))
                dve.wait_ge(num_mm, b + 1)
                dve.tensor_tensor(u_f[:, b], bank[6 + b][:], rden[:, b], ALU.mult).then_inc(u_ready, 1)
            dve.wait_ge(ld_mask, 16)
            dve.tensor_scalar(mask_b[:, :, 0:TK], mask_u[:, :, 0:TK], MASKED, None, ALU.mult)
            dve.memset(ones_b[:], 1.0).then_inc(mask_ready, 1)
            for b in range(NB):
                dve.wait_ge(att0_mm, b + 1)
                dve.wait_ge(a_bo_ready, b + 1)
                link(dve.tensor_tensor(r_t[:, b], by_tile(bank[4 + b][:]), a_bo[:, b], ALU.add))
                ln_stats(LN_R, b, r_t)
            dve.memset(v_a[:], 0.0)
            link(dve.memset(v_b[:], 0.0))
            for hq in range(HQ):
                c = head_col(hq) + HD
                dve.memset(v_a[:, :, hq * HG:(hq + 1) * HG, c:c + 1], 1.0)
                for g in range(HG):
                    last = dve.memset(v_b[KB * g:KB * g + KB, :, hq, GW * g + c:GW * g + c + 1], 1.0)
            last.then_inc(v_pad, 1)
            gamma = row[:, R_GAMMA:R_GAMMA + P]
            for b in range(NB):
                for j in range(NJ):
                    last = dve.scalar_tensor_tensor(out=y_t[:, b, j], in0=r_t[:, b, j],
                                                    scalar=mv[:, LN_R, b, j, 0:1], in1=gamma,
                                                    op0=ALU.subtract, op1=ALU.mult)
                link(last)
                dve.wait_ge(rstd_ready, LN_R * NB + b + 1)
                dve.wait_ge(x_beta_ready, b + 1)
                for j in range(NJ):
                    last = dve.scalar_tensor_tensor(out=x1[:, b, j], in0=y_t[:, b, j],
                                                    scalar=rstd[:, LN_R, b, j:j + 1], in1=x_beta[:, b, j],
                                                    op0=ALU.mult, op1=ALU.add)
                link(last)
                ln_stats(LN_X1, b, x1)
            for b in range(NB):
                ln_apply(LN_X1, b, x1, z_n).then_inc(z_ready, 1)
            for step in range(NB):
                dve.wait_ge(gates_act, 3 * step + 1)
                if step == 0:
                    dve.tensor_scalar(g_f[:, 0], g_act[:, 0, 0], 1.0, c0_half[:], ALU.add, ALU.mult)
                else:
                    dve.scalar_tensor_tensor(out=g_f[:, 1], in0=g_act[:, 1, 0], scalar=1.0, in1=cell[:, 0],
                                             op0=ALU.add, op1=ALU.mult)
                dve.wait_ge(gates_act, 3 * step + 3)
                link(dve.scalar_tensor_tensor(out=g_i[:, step], in0=g_act[:, step, 1], scalar=1.0,
                                              in1=g_act[:, step, 2], op0=ALU.add, op1=ALU.mult))
                dve.scalar_tensor_tensor(out=cell[:, step], in0=g_i[:, step], scalar=0.5 if step == 0 else 1.0,
                                         in1=g_f[:, step], op0=ALU.mult, op1=ALU.add).then_inc(cell_ready, 1)
                dve.wait_ge(cell_ready, step + 1)
            for b in range(NB):
                dve.wait_ge(h_tr, b + 1)
                dve.tensor_tensor(x2[:, b], by_tile(bank[6 + b][:]), x1[:, b], ALU.add).then_inc(x2_ready, 1)
                dve.wait_ge(x2_ready, b + 1)
                ln_stats(LN_X2, b, x2)
            for b in range(NB):
                ln_apply(LN_X2, b, x2, s_n).then_inc(s_ready, 1)
            for b in range(NB):
                dve.wait_ge(q1_mm, b + 1)
                link(dve.tensor_scalar(q1[:, b], bank[4 + b][:], col[:, C_BQ1:C_BQ1 + 1], QK_SCALE, ALU.add,
                                       ALU.mult))
                dve.tensor_copy(q_part[:, b, 0], q1[:, b]).then_inc(q_parts, 1)
                dve.wait_ge(q_parts, 3 * b + 1)
                link(dve.tensor_tensor(q_r1[:, b], q1[:, b], q_part[:, b, 0], ALU.subtract))
                dve.tensor_copy(q_part[:, b, 1], q_r1[:, b]).then_inc(q_parts, 1)
                dve.wait_ge(q_parts, 3 * b + 2)
                dve.tensor_tensor(q_part[:, b, 2], q_r1[:, b], q_part[:, b, 1], ALU.subtract).then_inc(q_parts, 1)

            def maxima(b, ring):
                n = b * NG
                for k, groups in enumerate(MAX_GROUPS):
                    for j in range(NJ):
                        for h0, nh in groups:
                            dve.wait_ge(score_mm, n + 1)
                            src = bank[ring[(n - b * NG) % len(ring)]][:, 0:nh * TK]
                            dve.tensor_reduce(nmax[:, b, j, h0:h0 + nh], src.rearrange("p (h k) -> p h k", k=TK),
                                              AX.X, ALU.max, negate=True).then_inc(max_taken, 1)
                            n += 1
                    h0, nh = HALVES[k]
                    whole, rest, part = nmax[:, b, :, h0:h0 + nh], nm_r1[:, b, :, h0:h0 + nh], nm_part[k][:, b]
                    dve.wait_ge(max_taken, n)
                    link(dve.tensor_copy(part[:, :, 0], whole))
                    link(dve.tensor_tensor(rest, whole, part[:, :, 0], ALU.subtract))
                    link(dve.tensor_copy(part[:, :, 1], rest))
                    dve.tensor_tensor(part[:, :, 2], rest, part[:, :, 1], ALU.subtract).then_inc(nm_parts, 1)

            def tail(b, piece):
                first, second = (bank[i] for i in PAIR[b])
                if piece == T_NORM:
                    dve.wait_ge(o_turned, b + 1)
                    view = [t[:].rearrange("p (j g c) -> p j g c", j=NJ, g=HG) for t in (first, second)]
                    for hq in range(HQ):
                        c = head_col(hq) + HD
                        last = dve.reciprocal(rsum[:, b, :, hq * HG:(hq + 1) * HG], view[hq // HQA][:, :, :, c])
                    link(last)
                    for j in range(NJ):
                        for hq in range(HQ):
                            c0 = head_col(hq)
                            dst = o_t[:, b, j, hq * HG * HD:(hq + 1) * HG * HD].rearrange("p (g d) -> p g d", d=HD)
                            last = dve.tensor_tensor(dst, view[hq // HQA][:, j, :, c0:c0 + HD],
                                                     rsum[:, b, j, hq * HG:(hq + 1) * HG]
                                                     .rearrange("p (g o) -> p g o", o=1)
                                                     .broadcast_to([P, HG, HD]), ALU.mult)
                    last.then_inc(o_ready, 1)
                elif piece == T_PROJ:
                    dve.wait_ge(att1_mm, b + 1)
                    dve.wait_ge(x2_bo_ready, b + 1)
                    dve.tensor_tensor(x3[:, b], by_tile(second[:]), x2_bo[:, b], ALU.add).then_inc(x3_ready, 1)
                    dve.wait_ge(x3_ready, b + 1)
                    ln_stats(LN_X3, b, x3)
                elif piece == T_IN:
                    ln_apply(LN_X3, b, x3, e_n).then_inc(e_ready, 1)
                elif piece == T_GATE:
                    dve.wait_ge(e_f_ready, b + 1)
                    dve.tensor_tensor(e_l[:, b], first[:], e_h[:, b].bitcast(F32), ALU.subtract)\
                       .then_inc(e_l_ready, 1)
                    dve.wait_ge(logit_mm, b + 1)
                    bg = row[:, R_BG:R_BG + E].rearrange("p (o e) -> p o e", o=1).broadcast_to([P, NJ, E])
                    link(dve.tensor_tensor(logit[:, b], second[:, 0:NJ * E].rearrange("p (j e) -> p j e", j=NJ),
                                           bg, ALU.add))
                    for j in range(NJ):
                        last = dve.max(top_v[:, b, j], logit[:, b, j])
                    link(last)
                    dve.tensor_tensor(gap[:, b], top_v[:, b, :, 1], top_v[:, b, :, 0], ALU.subtract)\
                       .then_inc(gap_ready, 1)
                    for j in range(NJ):
                        last = dve.max_index(top_i[:, b, j], top_v[:, b, j], logit[:, b, j])
                    link(last)
                    link(dve.tensor_copy(top_f[:, b], top_i[:, b]))
                    iota = iota_f[:].rearrange("p (o e) -> p o e", o=1).broadcast_to([P, NJ, E])

                    def pick(k):
                        return top_f[:, b, :, k:k + 1].broadcast_to([P, NJ, E])

                    def weight(k):
                        return w_top[:, b, k].rearrange("p (j o) -> p j o", o=1).broadcast_to([P, NJ, E])

                    dve.tensor_tensor(hit1[:, b], iota, pick(0), ALU.is_equal)
                    dve.tensor_tensor(hit2[:, b], iota, pick(1), ALU.is_equal)
                    dve.wait_ge(gap_exp, b + 1)
                    link(dve.tensor_scalar(gap_1[:, b], gap_e[:, b], 1.0, None, ALU.add))
                    link(dve.reciprocal(w_top[:, b, 0], gap_1[:, b]))
                    link(dve.tensor_tensor(w_top[:, b, 1], w_top[:, b, 0], gap_e[:, b], ALU.mult))
                    dve.tensor_tensor(hit1w[:, b], hit1[:, b], weight(0), ALU.mult)
                    link(dve.tensor_tensor(hit2w[:, b], hit2[:, b], weight(1), ALU.mult))
                    link(dve.tensor_tensor(comb[:, b], hit1w[:, b], hit2w[:, b], ALU.add))
                    link(dve.tensor_copy(comb_part[:, b, :, 0], comb[:, b]))
                    link(dve.tensor_tensor(comb_r[:, b], comb[:, b], comb_part[:, b, :, 0], ALU.subtract))
                    link(dve.tensor_copy(comb_part[:, b, :, 1], comb_r[:, b]))
                    dve.tensor_tensor(comb_part[:, b, :, 2], comb_r[:, b], comb_part[:, b, :, 1],
                                      ALU.subtract).then_inc(comb_ready, 1)

            def hidden(n):
                for c in range(HC):
                    g = n * HC + c
                    h = hid[:, g % NH]
                    dve.wait_ge(hid_full, g + 1)
                    dve.wait_ge(comb_b_ready, n + 1)
                    dve.tensor_tensor(h, h, comb_b[:, n % NCB], ALU.mult).then_inc(weighted, 1)
                    if c == 0:
                        dve.wait_ge(weighted, g + 1)
                        dve.tensor_copy(hid_h[:, g % NH], h).then_inc(hid_hi[0], 1)

            def hidden_lo(n):
                if not lo_on_pool(n % E, 1):
                    g = n * HC + 1
                    dve.wait_ge(hid_hi[1], n + 1)
                    dve.tensor_tensor(hid_l[:, g % NH], hid[:, g % NH], hid_h[:, g % NH].bitcast(F32),
                                      ALU.subtract).then_inc(hid_lo_dve, 1)

            def finish(b):
                dve.wait_ge(y_tr, b + 1)
                dve.tensor_tensor(res[:, b], by_tile(bank[PAIR[b][1]][:]), x3[:, b], ALU.add).then_inc(res_ready, 1)

            dve.tensor_copy(iota_f[:], iota_u[:])
            maxima(0, RING)
            maxima(1, PAIR[1])
            for k in range(T_COMB):
                tail(0, k)
            for n in range(NB * E + 1):
                if n < NB * E:
                    hidden(n)
                if n >= 1:
                    hidden_lo(n - 1)
                if n in TAIL_DVE:
                    tail(1, TAIL_DVE[n])
                if n == E + 3:
                    finish(0)
            finish(1)


def kernel(**inputs):
    import numpy as np
    import concourse.bacc as bacc
    from concourse.bass_utils import run_bass_kernel_spmd

    a = {k: np.asarray(v) for k, v in inputs.items()}

    def by_feature(m):
        return m.reshape(m.shape[:-1] + (H, HD)).swapaxes(-1, -2).reshape(m.shape)

    wk1, wv1 = a["L1_xattn_Wkv"][:, :P], a["L1_xattn_Wkv"][:, P:]
    bk1, bv1 = a["L1_xattn_bkv"][:P], a["L1_xattn_bkv"][P:]
    b1 = a["L1_ffn_b1"].reshape(E * HC, P)
    laid = {
        "x": a["x"],
        "ctxt": a["ctx_1024"].transpose(2, 0, 1),
        "mask": a["mask_BxS2_bk0"][None],
        "w_ctx": np.concatenate([a["L0_xattn_Wk"].T, a["L0_xattn_Wv"].T, wv1, by_feature(wk1)], axis=1),
        "w_l0": np.concatenate([a["L0_xattn_Wq"].T, a["L0_xattn_Wo"].T], axis=1),
        "w_ffn": np.concatenate([a["L0_ffn_" + n].T for n in W_FFN], axis=1),
        "w_l1": np.concatenate([by_feature(a["L1_xattn_Wq"]), a["L1_xattn_Wo"], a["L1_ffn_Wg"]], axis=1),
        "cols": np.stack([a["L0_xattn_bq"], a["L0_ffn_bf"], a["L0_ffn_bi"], a["L0_ffn_bc"], a["L0_ffn_in_c"],
                          a["L0_ffn_bo"], by_feature(bk1), by_feature(a["L1_xattn_bq"]), *b1], axis=1),
        "rows": np.concatenate([a["L0_xattn_bo"], a["L0_xattn_gamma"], a["L0_xattn_beta"], a["L1_xattn_bo"],
                                a["L1_ffn_bg"], a["L0_xattn_bk"], a["L0_xattn_bv"], bv1]),
        "w1": a["L1_ffn_W1"],
        "w2": a["L1_ffn_W2"],
        "b2": a["L1_ffn_b2"],
    }
    nc = bacc.Bacc("TRN2", target_bir_lowering=False, num_devices=1)
    arrays, args = {}, []
    for name, v in laid.items():
        v = np.ascontiguousarray(v)
        arrays[f"in_{name}"] = v
        args.append(nc.dram_tensor(f"in_{name}", v.shape, mybir.dt.from_np(v.dtype), kind="ExternalInput").ap())
    args.append(nc.dram_tensor("out_x", (NB, T, P), F32, kind="ExternalOutput").ap())
    two_blocks(nc, *args)
    r = run_bass_kernel_spmd(nc, [arrays], core_ids=[0])
    return r.results[0]["out_x"]
```

```python
from contextlib import ExitStack

import concourse.bass as bass
from concourse import mybir

P = 128
NB = 2
NJ = 4
T = NJ * P
TK = 154
KB = 32
TKP = P + KB
KR = TK - P
H = 16
HD = P // H
HG = 4
HQ = H // HG
GW = 32
HALVES = ((0, 9), (9, 7))
E = 8
HC = 2
BP = 64
EPS_LN = 1e-5
EPS_DEN = 1e-6
MASKED = -3e38
QK_SCALE = float(HD) ** -0.5
SLOTS = ((0, 0), (0, 1), (1, 0), (1, 1), (0, 2), (2, 0))
ROW_MASK = len(SLOTS) * HD
ROW_MAX = ROW_MASK + 1
ROWS_SCORE = ROW_MASK + 1
ROWS_ALL = ROW_MAX + 3

F32 = mybir.dt.float32
F32R = mybir.dt.float32r
BF16 = mybir.dt.bfloat16
U8 = mybir.dt.uint8
U32 = mybir.dt.uint32
ALU = mybir.AluOpType
ACT = mybir.ActivationFunctionType
AX = mybir.AxisListType

W_FFN = ("wf", "wi", "wc", "uf", "ui", "uc", "wo", "uo")
C_BQ0, C_BF, C_BI, C_BC, C_INC, C_BOF, C_BK1, C_BQ1, C_B1 = 0, 1, 2, 3, 4, 5, 6, 7, 8
N_COLS = C_B1 + E * HC
R_BO0, R_GAMMA, R_BETA, R_BO1, R_BG = 0, P, 2 * P, 3 * P, 4 * P
R_BK0, R_BV0, R_BV1 = R_BG + E, R_BG + E + P, R_BG + E + 2 * P
N_ROWS = R_BV1 + P

LN_X, LN_R, LN_X1, LN_X2, LN_X3 = range(5)
N_LN = 5
NJ_DVE = 2
T_NORM0, T_NORM1, T_NORM2, T_NORM3, T_TURN, T_PROJ, T_IN, T_GATE, T_PICK, T_COMB = range(10)
UNIT_PE = {1: (0, T_NORM0), 3: (0, T_NORM1), 4: (0, T_NORM2), 5: (0, T_NORM3), 7: (0, T_TURN), 9: (0, T_PROJ),
           11: (1, T_NORM0), 13: (0, T_IN), 15: (0, T_GATE), 18: (1, T_NORM1), 19: (0, T_COMB), 21: (1, T_NORM2)}
UNIT_ACT = {8: (0, T_PROJ), 13: (0, T_IN), 15: (0, T_GATE), 20: (0, T_COMB)}
UNIT_DVE = {1: (0, T_NORM0), 3: (0, T_NORM1), 4: (0, T_NORM2), 5: (0, T_NORM3), 9: (0, T_PROJ), 11: (1, T_NORM0),
            12: (0, T_IN), 15: (0, T_GATE), 16: (0, T_PICK), 18: (1, T_NORM1), 21: (1, T_NORM2)}
TAIL_PE = {1: T_TURN, 2: T_PROJ, 4: T_IN, 5: T_GATE, 7: T_COMB}
TAIL_ACT = {1: T_PROJ, 4: T_IN, 5: T_GATE, 7: T_COMB}
TAIL_DVE = {1: T_PROJ, 2: T_IN, 4: T_GATE, 5: T_PICK}
TAIL_LN = 2
LN_X3_UNIT = 10
SPLIT = (("AP", "--", "AP", "AP", "--"), ("AP", "--", "AP", "--", "AP"))
LAG = 4


def two_blocks(nc, x, ctxt, mask, w_ctx, w_l0, w_ffn, w_l1, cols, rows, w1, w2, b2, out):
    with ExitStack() as ctx:
        def sb(name, shape, dt=F32):
            return ctx.enter_context(nc.sbuf_tensor(name, shape, dt))

        bank = [ctx.enter_context(nc.psum_tensor(f"bank{i}", [P, 512], F32)) for i in range(8)]

        def sem(name):
            return ctx.enter_context(nc.semaphore(name))

        x_t = sb("x_t", [P, NB, NJ, P])
        ctx_t = sb("ctx_t", [P, NB, TKP])
        ctx_rep = sb("ctx_rep", [P, NB, HG, KB])
        mask_u = sb("mask_u", [1, NB, TKP], U8)
        mask_b = sb("mask_b", [1, NB, TKP], BF16)
        wc_s = sb("wc_s", [P, 4 * P])
        w0_s = sb("w0_s", [P, 2 * P])
        wf_s = sb("wf_s", [P, 8 * P])
        w3_s = sb("w3_s", [P, 2 * P + E])
        col = sb("col", [P, N_COLS])
        row = sb("row", [P, N_ROWS])
        w1_s = sb("w1_s", [P, E, HC * P])
        w2_s = w1_s[:].rearrange("p e (c d) -> p e c d", c=HC)
        w1_h = sb("w1_h", [P, E, HC * P], F32R)
        w1_l = sb("w1_l", [P, E, HC * P], F32R)
        w2_h = sb("w2_h", [P, E, HC, P], F32R)
        w2_l = sb("w2_l", [P, E, HC, P], F32R)
        b2_s = sb("b2_s", [3 * E, P])
        b2_r = sb("b2_r", [3 * E, P])
        b2_part = sb("b2_part", [3 * E, 3, P], BF16)
        pick_e = sb("pick_e", [3 * E, E, P], BF16)
        ident = sb("ident", [P, P])
        ident_b = sb("ident_b", [P, P], BF16)
        ones_b = sb("ones_b", [3, T], BF16)
        ones_f = sb("ones_f", [1, P])
        m_half = sb("m_half", [P, NJ])
        iota_u = sb("iota_u", [P, E], U32)
        iota_f = sb("iota_f", [P, E])
        bq0_1 = sb("bq0_1", [P, 1])
        bq0_neg = sb("bq0_neg", [P, 1])
        gate0 = sb("gate0", [P, 3])
        gate1 = sb("gate1", [P, 3])
        c0_half = sb("c0_half", [P, 1])
        eps_den = sb("eps_den", [P, 1])
        v_done = sb("v_done", [1, 1])
        o_done = sb("o_done", [1, 1])
        stats = sb("stats", [P, N_LN, NB, NJ, 6])
        mv = sb("mv", [P, N_LN, NB, NJ, 2])
        vare = sb("vare", [P, N_LN, NB, NJ])
        rstd = sb("rstd", [P, N_LN, NB, NJ])
        neg_mean = sb("neg_mean", [P, N_LN, NB, NJ])
        mean_rstd = sb("mean_rstd", [P, N_LN, NB, NJ])
        k0 = sb("k0", [P, NB, 2, P])
        k0_b = sb("k0_b", [P, NB, 2, P])
        k0_m = sb("k0_m", [P, NB, 2, P])
        k0_e = sb("k0_e", [P, NB, 2, P])
        v0 = sb("v0", [P, NB, 2, P + 1])
        kv0 = sb("kv0", [P, NB, P + 1])
        a_n = sb("a_n", [P, NB, NJ, P])
        y_t = sb("y_t", [P, NB, NJ, P])
        x_beta = sb("x_beta", [P, NB, NJ, P])
        a_f = sb("a_f", [P, NB, T])
        q_m = sb("q_m", [P, NB, T])
        q_e = sb("q_e", [P, NB, T])
        q0 = sb("q0", [P, NB, T])
        den = q_e
        rden = q_m
        r_t = sb("r_t", [P, NB, NJ, P])

        x1 = sb("x1", [P, NB, NJ, P])
        z_n = a_n
        z_f = q0
        g_act = sb("g_act", [P, NB, 3, T])
        g_f = q_m
        g_i = q_e
        u_f = g_act[:, :, 0]
        cell = y_t[:].rearrange("p b j d -> p b (j d)")
        uo_half = sb("uo_half", [P, P])
        h_f = cell
        x2 = x_t
        x2_bo = x_beta
        s_n = a_n
        s_f = a_f
        q1 = q_m
        q_r1 = q_e
        hid_h = sb("hid_h", [P, NB * 3, T], F32R)
        hid_l = sb("hid_l", [P, NB * 3, T], F32R)
        q_part = g_act[:, 0].bitcast(BF16).rearrange("p s (b t) -> p b s t", b=NB)
        q_stack = sb("q_stack", [P, H, T], BF16)
        k1 = g_act[:, 0, 1, 0:NB * TKP].rearrange("p (b k) -> p b k", b=NB)
        k_r1 = g_act[:, 0, 2, 0:NB * TKP].rearrange("p (b k) -> p b k", b=NB)
        k_part = g_act[:, 1, 1].bitcast(BF16)[:, 0:NB * 3 * TKP].rearrange("p (b s k) -> p b s k", b=NB, s=3)
        k_stack = sb("k_stack", [P, H, TKP], BF16)
        v1 = k0_m
        v1f = k0_e
        v_a = sb("v_a", [P, NB, HQ, HG, HG * GW], F32R)
        v_b = sb("v_b", [P, NB, HQ, HG * GW], F32R)
        nmax = sb("nmax", [P, NB, NJ, H])
        nm_r1 = sb("nm_r1", [P, NB, NJ, H])
        nm_part = [sb(f"nm_part{k}", [P, NB, NJ, 3, n], BF16) for k, (_, n) in enumerate(HALVES)]
        nm_f = [sb(f"nm_f{k}", [3 * n, T], BF16) for k, (_, n) in enumerate(HALVES)]
        NPR = NB * 3
        prob = g_act[:].rearrange("p s g t -> p (s g) t")
        prob_h, prob_l = hid_h, hid_l
        o_ev = ((q_m[:, 0], q_m[:, 1], q_e[:, 0], q_e[:, 1]), (a_f[:, 0], a_f[:, 1], cell[:, 0], cell[:, 1]))
        o_sum = r_t[:].rearrange("p b j d -> p b (j d)").rearrange("p b (q n d) -> p b q n d", q=HQ, d=HD)
        rsum = sb("rsum", [P, NB, HQ, NJ * HG])
        o_t = z_n
        o_f = z_f
        x3 = r_t
        e_n = z_n
        e_f = z_f
        e_h = sb("e_h", [P, NB, T], F32R)
        e_l = sb("e_l", [P, NB, T], F32R)
        logit = sb("logit", [P, NB, NJ, E])
        top_v = sb("top_v", [P, NB, NJ, E])
        top_i = sb("top_i", [P, NB, NJ, E], U32)
        top_f = sb("top_f", [P, NB, NJ, E])
        gap = sb("gap", [P, NB, NJ])
        gap_e = sb("gap_e", [P, NB, NJ])
        gap_1 = sb("gap_1", [P, NB, NJ])
        w_top = sb("w_top", [P, NB, 2, NJ])
        hit1 = sb("hit1", [P, NB, NJ, E])
        hit2 = sb("hit2", [P, NB, NJ, E])
        hit1w = sb("hit1w", [P, NB, NJ, E])
        hit2w = sb("hit2w", [P, NB, NJ, E])
        comb = sb("comb", [P, NB, NJ, E])
        comb_r = sb("comb_r", [P, NB, NJ, E])
        comb_part = sb("comb_part", [P, NB, NJ, 3, E], BF16)
        comb_f = k0[0:3 * E].rearrange("p b c d -> p (b c d)").bitcast(BF16).rearrange("p (b t) -> p b t", b=NB)
        NCB = 3
        comb_b = w1_s[:].rearrange("p e h -> p (e h)")[:, 0:NCB * T].rearrange("p (n t) -> p n t", t=T)
        NH = NPR
        hid = prob
        y_f = q_m
        res = x1

        ld_x = [sem(f"ld_x{b}") for b in range(NB)]
        ld_ctx = sem("ld_ctx")
        ld_row = sem("ld_row")
        ld_col = sem("ld_col")
        ld_mask = sem("ld_mask")
        ld_b2 = sem("ld_b2")
        ld_w0 = sem("ld_w0")
        ld_wf = sem("ld_wf")
        ld_w3 = sem("ld_w3")
        ld_w1 = sem("ld_w1")
        ld_w2 = sem("ld_w2")
        pool_step = sem("pool_step")
        consts_ready = sem("consts_ready")
        dve_step = sem("dve_step")
        eps_ready = sem("eps_ready")
        ones_ready = sem("ones_ready")
        bq0_ready = sem("bq0_ready")
        v_pad = sem("v_pad")
        v_ready = sem("v_ready")
        k1_ready = sem("k1_ready")
        den_ready = sem("den_ready")
        rden_ready = sem("rden_ready")
        b2_ready = sem("b2_ready")
        pad_ready = sem("pad_ready")
        mask_ready = sem("mask_ready")
        ctx_rep_ready = sem("ctx_rep_ready")
        var_ready = sem("var_ready")
        mean_ready = sem("mean_ready")
        rstd_ready = sem("rstd_ready")
        mean_rstd_ready = sem("mean_rstd_ready")
        ctx_a_mm = sem("ctx_a_mm")
        ctx_b_mm = sem("ctx_b_mm")
        k1_mm = sem("k1_mm")
        k0_neg = sem("k0_neg")
        k0_exp = sem("k0_exp")
        k0_ready = sem("k0_ready")
        v0_ready = sem("v0_ready")
        v1_ready = sem("v1_ready")
        kv0_mm = sem("kv0_mm")
        kv0_ready = sem("kv0_ready")
        gate_c_mm = sem("gate_c_mm")
        gate_c_ready = sem("gate_c_ready")
        k_parts = sem("k_parts")
        k_stacked = [sem(f"k_stacked{b}") for b in range(NB)]
        a_ready = sem("a_ready")
        a_ready_act = sem("a_ready_act")
        a_tr = sem("a_tr")
        a_f_ready = sem("a_f_ready")
        y_ready = sem("y_ready")
        q0_mm = sem("q0_mm")
        q0_neg = sem("q0_neg")
        q0_exp = sem("q0_exp")
        q0_ready = sem("q0_ready")
        num_mm = sem("num_mm")
        u_ready = sem("u_ready")
        att0_mm = sem("att0_mm")
        x_beta_ready = sem("x_beta_ready")
        z_ready = sem("z_ready")
        z_ready_act = sem("z_ready_act")
        z_tr = sem("z_tr")
        z_f_ready = sem("z_f_ready")
        gates_mm = sem("gates_mm")
        gates_act = sem("gates_act")
        cell_ready = sem("cell_ready")
        uo_ready = sem("uo_ready")
        h_mm = sem("h_mm")
        h_act = sem("h_act")
        h_tr = sem("h_tr")
        x2_ready = sem("x2_ready")
        s_ready = sem("s_ready")
        s_ready_act = sem("s_ready_act")
        s_tr = sem("s_tr")
        s_f_ready = sem("s_f_ready")
        q1_mm = sem("q1_mm")
        q_parts = sem("q_parts")
        q_stacked = [sem(f"q_stacked{b}") for b in range(NB)]
        score_mm = sem("score_mm")
        max_taken = sem("max_taken")
        nm_parts = sem("nm_parts")
        nm_tr = sem("nm_tr")
        nm_f_ready = sem("nm_f_ready")
        nm_stacked = [[sem(f"nm_stacked{b}_{k}") for k in range(2)] for b in range(NB)]
        st_mm = sem("st_mm")
        prob_ready = sem("prob_ready")
        prob_hi_act = sem("prob_hi_act")
        prob_hi_dve = sem("prob_hi_dve")
        prob_lo_pool = sem("prob_lo_pool")
        prob_lo_dve = sem("prob_lo_dve")
        pv_mm = sem("pv_mm")
        o_ev_ready = sem("o_ev_ready")
        o_normed = sem("o_normed")
        o_summed = sem("o_summed")
        o_turned = sem("o_turned")
        o_ready = sem("o_ready")
        o_tr = sem("o_tr")
        o_f_ready = sem("o_f_ready")
        att1_mm = sem("att1_mm")
        x2_bo_ready = sem("x2_bo_ready")
        x3_ready = sem("x3_ready")
        w_hi = sem("w_hi")
        w_lo = sem("w_lo")
        e_ready = sem("e_ready")
        e_tr = sem("e_tr")
        e_f_ready = sem("e_f_ready")
        e_h_ready = sem("e_h_ready")
        e_l_ready = sem("e_l_ready")
        logit_mm = sem("logit_mm")
        gap_ready = sem("gap_ready")
        top_ready = sem("top_ready")
        gap_exp = sem("gap_exp")
        comb_ready = sem("comb_ready")
        comb_tr = sem("comb_tr")
        comb_f_ready = sem("comb_f_ready")
        comb_b_mm = sem("comb_b_mm")
        comb_b_ready = sem("comb_b_ready")
        h1_mm = sem("h1_mm")
        hid_full = sem("hid_full")
        weighted = sem("weighted")
        hid_hi = [sem(f"hid_hi{c}") for c in range(HC)]
        hid_lo_pool = sem("hid_lo_pool")
        hid_lo_dve = sem("hid_lo_dve")
        y_mm = sem("y_mm")
        y_f_ready = sem("y_f_ready")
        y_tr = sem("y_tr")
        res_ready = sem("res_ready")
        stored = sem("stored")

        UPB = H + HQ
        UNITS = [(hq, i) for hq in range(HQ) for i in range(HG + 1)]
        UNITS_ALL = NB * UPB
        RING = (0, 1, 6, 7)
        PV = (4, 5)
        TB = (2, 3)
        XP = ((4, 5), (2, 3))
        OUT = ((0, slice(0, NJ), XP[0][1]), (1, slice(0, NJ // 2), XP[1][1]), (1, slice(NJ // 2, NJ), XP[0][0]))
        GROUPS = [(b, k, j, g, min(3, h0 + n - g)) for b in range(NB) for k, (h0, n) in enumerate(HALVES)
                  for j in range(NJ) for g in range(h0, h0 + n, 3)]
        END = [[sum(v[:2] <= (b, k) for v in GROUPS) for k in range(2)] for b in range(NB)]
        ITEMS = []
        for n in range(END[0][0], len(GROUPS)):
            ITEMS.append(n)
            for b in range(NB):
                for k in range(2):
                    if n + 1 == END[b][k] + 3:
                        ITEMS.append((b, k))
        ITEMS.append((1, 1))
        ALONE = 7
        PER_UNIT = {u: 1 + (u % 2 if u < UPB else 0) for u in range(UNITS_ALL)}

        def items_after(u):
            lo = ALONE + sum(PER_UNIT[v] for v in range(u)) if u >= 0 else 0
            return range(lo, min(len(ITEMS), lo + (PER_UNIT[u] if u >= 0 else ALONE)))

        def bank_of(n):
            return RING[n % 4] if n < END[0][0] else TB[ITEMS.index(n) % 2]

        def hi_by(u):
            return SPLIT[u // UPB][u % UPB % (HG + 1)][0]

        def lo_by(u):
            return SPLIT[u // UPB][u % UPB % (HG + 1)][1]

        def hi_counts(n):
            at = [hi_by(u) for u in range(n)]
            return at.count("A"), at.count("D")

        def p_lo_counts(n):
            at = [lo_by(u) for u in range(n)]
            return at.count("P"), at.count("D")

        def lo_on_pool(n, c):
            return n != NB * E - 1 and (c == 0 or n % 2 == 0 or n < E)

        def lo_counts(n):
            at = [lo_on_pool(v // HC, v % HC) for v in range(n)]
            return sum(at), n - sum(at)

        def wait_both(engine, sem_a, sem_b, counts):
            for s_, n in zip((sem_a, sem_b), counts):
                if n:
                    engine.wait_ge(s_, n)

        block = ctx.enter_context(nc.Block())

        @block.sync
        def _(sp):
            for b in range(NB):
                sp.dma_start(x_t[:, b], x[b].rearrange("(p j) d -> p j d", j=NJ)).then_inc(ld_x[b], 16)
            sp.dma_start(row[:], rows.partition_broadcast(P)).then_inc(ld_row, 16)
            sp.dma_start(w0_s[:], w_l0).then_inc(ld_w0, 16)
            sp.dma_start(wf_s[:], w_ffn).then_inc(ld_wf, 16)
            sp.dma_start(w3_s[:], w_l1).then_inc(ld_w3, 16)
            for p in range(3):
                sp.dma_start(b2_s[p * E:(p + 1) * E], b2).then_inc(ld_b2, 16)
            sp.dma_start(w1_s[:], w1.rearrange("e d h -> d e h")).then_inc(ld_w1, 16)
            sp.wait_ge(mask_ready, 1)
            for b in range(NB):
                sp.dma_start(q_stack[BP * b + ROW_MASK:BP * b + ROW_MASK + 1],
                             ones_b[0:1, :].rearrange("p (o t) -> p o t", o=1).broadcast_to([1, H, T]))\
                  .then_inc(q_stacked[b], 16)
                sp.dma_start(k_stack[BP * b + ROW_MAX:BP * b + ROW_MAX + 3],
                             ones_b[:, 0:TKP].rearrange("p (o t) -> p o t", o=1).broadcast_to([3, H, TKP]))\
                  .then_inc(k_stacked[b], 16)
            sp.wait_ge(k_parts, 1)
            for b in range(NB):
                for s, (_, kp) in enumerate(SLOTS):
                    sp.dma_start(k_stack[BP * b + HD * s:BP * b + HD * s + HD], k_part[:, b, kp])\
                      .then_inc(k_stacked[b], 16)
                sp.dma_start(k_stack[BP * b + ROW_MASK:BP * b + ROW_MASK + 1],
                             mask_b[0:1, b:b + 1, :].broadcast_to([1, H, TKP])).then_inc(k_stacked[b], 16)
            for b in range(NB):
                for part in range(3):
                    sp.wait_ge(q_parts, 3 * b + part + 1)
                    for s, (qp, _) in enumerate(SLOTS):
                        if qp == part:
                            sp.dma_start(q_stack[BP * b + HD * s:BP * b + HD * s + HD], q_part[:, b, qp])\
                              .then_inc(q_stacked[b], 16)
            for b in range(NB):
                for k, (h0, n) in enumerate(HALVES):
                    sp.wait_ge(nm_f_ready, 2 * b + k + 1)
                    sp.dma_start(q_stack[BP * b + ROW_MAX:BP * b + ROW_MAX + 3, h0:h0 + n], nm_f[k][:])\
                      .then_inc(nm_stacked[b][k], 16)
            for k, (b, tiles, _) in enumerate(OUT):
                sp.wait_ge(res_ready, k + 1)
                sp.dma_start(out[b].rearrange("(p j) d -> p j d", j=NJ)[:, tiles], res[:, b, tiles]).then_inc(stored, 16)
            sp.wait_ge(stored, 16 * len(OUT))

        @block.gpsimd
        def _(pool):
            steps = [0]

            def link(ins):
                steps[0] += 1
                ins.then_inc(pool_step, 1)
                pool.wait_ge(pool_step, steps[0])

            link(pool.memset(ident[:], 0.0))
            link(pool.affine_select(out=ident[:], in_=ident[:], compare_op=ALU.not_equal, fill=1.0,
                                    base=0, pattern=[[-1, P]], channel_multiplier=1))
            pool.memset(m_half[:], -0.5).then_inc(consts_ready, 1)
            pool.tensor_copy(ident_b[:], ident[:]).then_inc(consts_ready, 1)
            pool.iota(iota_u[:], pattern=[[1, E]], base=0, channel_multiplier=0).then_inc(consts_ready, 1)
            pool.wait_ge(consts_ready, 3)

            def rstd_of(n, b):
                k = n * NB + b
                pool.wait_ge(var_ready, k + 1)
                pool.tensor_tensor(rstd[:, n, b], vare[:, n, b], m_half[:], ALU.pow).then_inc(rstd_ready, 1)
                pool.wait_ge(rstd_ready, k + 1)
                pool.wait_ge(mean_ready, k + 1)
                pool.tensor_tensor(mean_rstd[:, n, b], neg_mean[:, n, b], rstd[:, n, b], ALU.mult)\
                    .then_inc(mean_rstd_ready, 1)

            def weight_lo(k):
                pool.wait_ge(w_hi, k + 1)
                w, h, lo = (w1_s, w1_h, w1_l) if k < 4 else (w2_s, w2_h, w2_l)
                s = slice(2 * (k % 4), 2 * (k % 4) + 2)
                pool.tensor_tensor(lo[:, s], w[:, s], h[:, s].bitcast(F32), ALU.subtract).then_inc(w_lo, 1)

            def add_rows(dst, src, off, b, done):
                v = row[:, off:off + P].rearrange("p (o d) -> p o d", o=1).broadcast_to([P, NJ, P])
                pool.tensor_tensor(dst[:, b], src[:, b], v, ALU.add).then_inc(done, 1)

            for b in range(NB):
                rstd_of(LN_X, b)
            pool.wait_ge(ld_row, 16)
            for b in range(NB):
                pool.wait_ge(ld_x[b], 16)
                add_rows(x_beta, x_t, R_BETA, b, x_beta_ready)
            pool.wait_ge(k1_ready, 1)
            link(pool.tensor_copy(k_part[:, :, 0], k1[:]))
            link(pool.tensor_tensor(k_r1[:], k1[:], k_part[:, :, 0], ALU.subtract))
            link(pool.tensor_copy(k_part[:, :, 1], k_r1[:]))
            pool.tensor_tensor(k_part[:, :, 2], k_r1[:], k_part[:, :, 1], ALU.subtract).then_inc(k_parts, 1)
            for b in range(NB):
                rstd_of(LN_R, b)
            for b in range(NB):
                rstd_of(LN_X1, b)
            pool.wait_ge(v_pad, 1)
            for b in range(NB):
                pool.wait_ge(v1_ready, b + 1)
                bv = row[:, R_BV1:R_BV1 + P].rearrange("p (o d) -> p o d", o=1).broadcast_to([P, 2, P])
                link(pool.tensor_tensor(v1f[:, b], v1[:, b], bv, ALU.add))
                for g in range(HG):
                    whole = v1f[:, b, 0].rearrange("p (q g d) -> p q g d", g=HG, d=HD)[:, :, g]
                    hi = v_a[:, b, :, g, GW * g:GW * g + HD]
                    link(pool.tensor_copy(hi, whole))
                    link(pool.tensor_tensor(v_a[:, b, :, g, GW * g + HD + 1:GW * g + 2 * HD + 1], whole,
                                            hi.bitcast(F32), ALU.subtract))
                    q = slice(KB * g, KB * g + KB)
                    whole = v1f[q, b, 1].rearrange("p (q g d) -> p q g d", g=HG, d=HD)[:, :, g]
                    hi = v_b[q, b, :, GW * g:GW * g + HD]
                    link(pool.tensor_copy(hi, whole))
                    link(pool.tensor_tensor(v_b[q, b, :, GW * g + HD + 1:GW * g + 2 * HD + 1], whole,
                                            hi.bitcast(F32), ALU.subtract))
            pool.memset(v_done[:], 0.0).then_inc(v_ready, 1)
            for k in range(0, 4):
                weight_lo(k)
            pool.wait_ge(w_lo, 4)
            pool.dma_start(w2_s[:], w2.rearrange("e (c p) d -> p e c d", p=P)).then_inc(ld_w2, 16)
            for b in range(NB):
                rstd_of(LN_X2, b)
            for b in range(NB):
                add_rows(x2_bo, x2, R_BO1, b, x2_bo_ready)
            def rows_of(k):
                return ident[0:3 * E, k * E:(k + 1) * E].rearrange("p (e o) -> p e o", o=1)\
                    .broadcast_to([3 * E, E, P])
            link(pool.tensor_tensor(pick_e[:], rows_of(0), rows_of(1), ALU.add))
            link(pool.tensor_tensor(pick_e[:], pick_e[:], rows_of(2), ALU.add))
            pool.wait_ge(ld_b2, 48)
            link(pool.tensor_copy(b2_part[:, 0], b2_s[:]))
            link(pool.tensor_tensor(b2_r[:], b2_s[:], b2_part[:, 0], ALU.subtract))
            link(pool.tensor_copy(b2_part[:, 1], b2_r[:]))
            pool.tensor_tensor(b2_part[:, 2], b2_r[:], b2_part[:, 1], ALU.subtract).then_inc(b2_ready, 1)
            for k in range(4, 8):
                weight_lo(k)

            def hidden_lo(b, e):
                for c in range(HC):
                    if not lo_on_pool(b * E + e, c):
                        continue
                    g = (b * E + e) * HC + c
                    pool.wait_ge(hid_hi[c], b * E + e + 1)
                    if g >= NH:
                        pool.wait_ge(y_mm, (g - NH) // HC + 1)
                    pool.tensor_tensor(hid_l[:, g % NH], hid[:, g % NH], hid_h[:, g % NH].bitcast(F32),
                                       ALU.subtract).then_inc(hid_lo_pool, 1)

            for u in range(UNITS_ALL):
                if u == UPB + LN_X3_UNIT:
                    rstd_of(LN_X3, 0)
                if lo_by(u) != "P":
                    continue
                n_act, n_dve = hi_counts(u + 1)
                if hi_by(u) == "A":
                    pool.wait_ge(prob_hi_act, n_act)
                else:
                    pool.wait_ge(prob_hi_dve, n_dve)
                if u >= NPR:
                    pool.wait_ge(pv_mm, u - NPR + 1)
                pool.tensor_tensor(prob_l[:, u % NPR], prob[:, u % NPR], prob_h[:, u % NPR].bitcast(F32),
                                   ALU.subtract).then_inc(prob_lo_pool, 1)
            for e in range(E):
                if e == TAIL_LN:
                    rstd_of(LN_X3, 1)
                hidden_lo(0, e)
            for e in range(E):
                hidden_lo(1, e)

        @block.scalar
        def _(act):
            act.dma_start(ctx_t[:, :, 0:TK], ctxt).then_inc(ld_ctx, 16)
            act.dma_start(wc_s[:], w_ctx).then_inc(ld_ctx, 16)
            act.dma_start(col[:], cols).then_inc(ld_col, 16)
            act.dma_start(mask_u[:, :, 0:TK], mask).then_inc(ld_mask, 16)

            def copy_out(src, dst, ready, n, done):
                act.wait_ge(ready, n)
                nc.scalar.activation(dst, src, ACT.Copy).then_inc(done, 1)

            def weight_hi(k):
                act.wait_ge(ld_w1 if k < 4 else ld_w2, 16)
                w, h = (w1_s, w1_h) if k < 4 else (w2_s, w2_h)
                s = slice(2 * (k % 4), 2 * (k % 4) + 2)
                nc.scalar.activation(h[:, s], w[:, s], ACT.Copy).then_inc(w_hi, 1)

            def values_out(b):
                act.wait_ge(v0_ready, b + 1)
                nc.scalar.activation(v1[:, b, 0], bank[b][:, 2 * P:3 * P], ACT.Copy)
                nc.scalar.activation(v1[:, b, 1], bank[2 + b][:, 2 * P:3 * P], ACT.Copy).then_inc(v1_ready, 1)

            def normalise(n, b, src, dst, ready, first=NJ_DVE):
                act.wait_ge(mean_rstd_ready, n * NB + b + 1)
                for j in range(first, NJ):
                    last = nc.scalar.activation(dst[:, b, j], src(b, j), ACT.Identity,
                                                bias=mean_rstd[:, n, b, j:j + 1], scale=rstd[:, n, b, j:j + 1])
                last.then_inc(ready, 1)

            def key_exp(b):
                act.wait_ge(k0_neg, b + 1)
                nc.scalar.activation(k0_e[:, b], k0_m[:, b], ACT.Exp).then_inc(k0_exp, 1)

            def query_exp(b):
                act.wait_ge(q0_mm, b + 1)
                if b == 0:
                    act.wait_ge(bq0_ready, 1)
                nc.scalar.activation(q_m[:, b], bank[6 + b][:], ACT.Relu, bias=bq0_neg[:], scale=-1.0)\
                  .then_inc(q0_neg, 1)
                act.wait_ge(q0_neg, b + 1)
                nc.scalar.activation(q_e[:, b], q_m[:, b], ACT.Exp, scale=-1.0).then_inc(q0_exp, 1)

            def denominator(b):
                act.wait_ge(kv0_ready, b + 1)
                act.wait_ge(q0_ready, b + 1)
                nc.scalar.activation(den[:, b], q0[:, b], ACT.Identity, bias=eps_den[:],
                                     scale=kv0[:, b, P:P + 1]).then_inc(den_ready, 1)

            act.wait_ge(eps_ready, 1)
            nc.scalar.activation(ones_f[:], eps_den[0:1, :].broadcast_to([1, P]), ACT.Exp, scale=0.0)\
              .then_inc(ones_ready, 1)
            for b in range(NB):
                normalise(LN_X, b, lambda b, j: x_t[:, b, j], a_n, a_ready_act)
            key_exp(0)
            copy_out(bank[6][:], a_f[:, 0], a_tr, 1, a_f_ready)
            query_exp(0)
            key_exp(1)
            copy_out(bank[7][:], a_f[:, 1], a_tr, 2, a_f_ready)
            denominator(0)
            query_exp(1)
            values_out(0)
            values_out(1)
            denominator(1)
            act.wait_ge(k1_mm, 1)
            act.wait_ge(ld_col, 16)
            nc.scalar.activation(k1[:], bank[0][:, 0:NB * TKP].rearrange("p (b k) -> p b k", b=NB), ACT.Identity,
                                 bias=col[:, C_BK1:C_BK1 + 1], scale=1.0).then_inc(k1_ready, 1)
            act.wait_ge(ld_wf, 16)
            nc.scalar.activation(uo_half[:], wf_s[:, 7 * P:8 * P], ACT.Copy, scale=0.5).then_inc(uo_ready, 1)
            for k in range(4):
                weight_hi(k)
            normalise(LN_R, 1, lambda b, j: bank[4 + b][:, j * P:(j + 1) * P], y_t, y_ready, 0)
            for b in range(NB):
                normalise(LN_X1, b, lambda b, j: x1[:, b, j], z_n, z_ready_act)
                if b == 0:
                    copy_out(bank[6][:], z_f[:, 0], z_tr, 1, z_f_ready)
            for b in range(NB):
                act.wait_ge(k_stacked[b], 16 * (len(SLOTS) + 2))
            for step in range(NB):
                bias = gate0 if step == 0 else gate1
                for g in range(3):
                    if step == 0 and g == 2:
                        copy_out(bank[7][:], z_f[:, 1], z_tr, 2, z_f_ready)
                    act.wait_ge(gates_mm, 3 * step + g + 1)
                    nc.scalar.activation(g_act[:, step, g], bank[3 * step + g][:], ACT.Tanh,
                                         bias=bias[:, g:g + 1], scale=1.0 if g == 2 else 0.5).then_inc(gates_act, 1)
            for b in range(NB):
                act.wait_ge(h_mm, b + 1)
                nc.scalar.activation(h_f[:, b], bank[b][:], ACT.Tanh, bias=col[:, C_BOF:C_BOF + 1],
                                     scale=1.0).then_inc(h_act, 1)
            for b in range(NB):
                normalise(LN_X2, b, lambda b, j: x2[:, b, j], s_n, s_ready_act)
                copy_out(bank[2 + b][:], s_f[:, b], s_tr, b + 1, s_f_ready)
            for k in range(4, 8):
                weight_hi(k)

            def max_out(b, k):
                n = 3 * HALVES[k][1]
                if b == 1:
                    act.wait_ge(nm_stacked[0][k], 16)
                src = bank[TB[ITEMS.index((b, k)) % 2]]
                copy_out(src[0:n, 0:T // 2].bitcast(BF16), nm_f[k][:], nm_tr, 2 * b + k + 1, nm_f_ready)

            def exps(u):
                act.wait_ge(st_mm, u + 1)
                if u >= NPR:
                    if hi_by(u - NPR) == "-":
                        act.wait_ge(pv_mm, u - NPR + 1)
                    else:
                        wait_both(act, prob_lo_pool, prob_lo_dve, p_lo_counts(u - NPR + 1))
                nc.scalar.activation(prob[:, u % NPR], bank[RING[u % 4]][:], ACT.Exp).then_inc(prob_ready, 1)

            def prob_hi(u):
                if hi_by(u) == "A":
                    act.wait_ge(prob_ready, u + 1)
                    if u >= NPR:
                        act.wait_ge(pv_mm, u - NPR + 1)
                    nc.scalar.activation(prob_h[:, u % NPR], prob[:, u % NPR], ACT.Copy).then_inc(prob_hi_act, 1)

            def group_out(m):
                b, hq = divmod(m, HQ)
                act.wait_ge(pv_mm, b * UPB + (hq + 1) * (HG + 1))
                nc.scalar.activation(o_ev[b][hq], bank[PV[m % 2]][:], ACT.Copy).then_inc(o_ev_ready, 1)

            def tail(b, piece):
                first = bank[TB[0]][:]
                if piece == T_PROJ:
                    copy_out(first, o_f[:, b], o_tr, b + 1, o_f_ready)
                elif piece == T_IN:
                    copy_out(first, e_h[:, b], e_tr, b + 1, e_h_ready)
                    nc.scalar.activation(e_f[:, b], first, ACT.Copy).then_inc(e_f_ready, 1)
                elif piece == T_GATE:
                    act.wait_ge(gap_ready, b + 1)
                    nc.scalar.activation(gap_e[:, b], gap[:, b], ACT.Exp).then_inc(gap_exp, 1)
                elif piece == T_COMB:
                    copy_out(bank[TB[0]][0:3 * E, 0:T // 2].bitcast(BF16), comb_f[:, b], comb_tr, b + 1,
                             comb_f_ready)

            def spread_comb(n):
                b = n // E
                act.wait_ge(comb_b_mm, n + 1)
                if n >= NCB:
                    act.wait_ge(weighted, (n - NCB + 1) * HC)
                nc.scalar.activation(comb_b[:, n % NCB], bank[XP[b][1]][:], ACT.Copy).then_inc(comb_b_ready, 1)

            def hidden(n):
                b, e = divmod(n, E)
                for c in range(HC):
                    g = n * HC + c
                    act.wait_ge(h1_mm, g + 1)
                    if g >= NH:
                        act.wait_ge(y_mm, (g - NH) // HC + 1)
                        n_pool, n_dve = lo_counts(g - NH + 1)
                        act.wait_ge(hid_lo_pool, n_pool)
                        if n_dve:
                            act.wait_ge(hid_lo_dve, n_dve)
                    v = e * HC + c
                    nc.scalar.activation(hid[:, g % NH], bank[RING[g % 4]][:], ACT.Relu,
                                         bias=col[:, C_B1 + v:C_B1 + v + 1], scale=1.0).then_inc(hid_full, 1)

            def hidden_hi(n):
                g = n * HC + 1
                act.wait_ge(weighted, g + 1)
                nc.scalar.activation(hid_h[:, g % NH], hid[:, g % NH], ACT.Copy).then_inc(hid_hi[1], 1)

            act.wait_ge(q_stacked[1], 16 * (len(SLOTS) + 1))
            for u in range(-1, UNITS_ALL + LAG + 1):
                if 0 <= u < UNITS_ALL:
                    exps(u)
                if 0 <= u - 1 < UNITS_ALL:
                    prob_hi(u - 1)
                if u < UNITS_ALL:
                    for i in items_after(u):
                        if isinstance(ITEMS[i], tuple):
                            max_out(*ITEMS[i])
                if u == UNITS_ALL + 2:
                    hidden(0)
                m, late = divmod(u - LAG - 1, HG + 1)
                if late == HG and m >= 0:
                    group_out(m)
                if u - UPB in UNIT_ACT:
                    tail(*UNIT_ACT[u - UPB])
            for n in range(NB * E + 1):
                if n < NB * E:
                    spread_comb(n)
                    if n > 0:
                        hidden(n)
                if TAIL_ACT.get(n) == T_COMB:
                    tail(1, T_COMB)
                if n >= 1:
                    hidden_hi(n - 1)
                if n in TAIL_ACT and TAIL_ACT[n] != T_COMB:
                    tail(1, TAIL_ACT[n])
                if n == E + 2:
                    copy_out(bank[XP[0][0]][:], y_f[:, 0], y_mm, E, y_f_ready)
            for k, (_, tiles, _) in enumerate(OUT[1:]):
                c = slice(tiles.start * P, tiles.stop * P)
                copy_out(bank[XP[1][0]][:, c], y_f[:, 1, c], y_mm, NB * E, y_f_ready)

        @block.tensor
        def _(pe):
            def transposes(dst, src, done):
                for j in range(NJ):
                    last = pe.transpose(dst[:, j * P:(j + 1) * P], src[:, j], ident[:])
                last.then_inc(done, 1)

            pe.wait_ge(ld_ctx, 32)
            pe.wait_ge(pad_ready, 1)
            for b in range(NB):
                pe.matmul(bank[b][:, 0:3 * P], ctx_t[:, b, 0:P], wc_s[:, 0:3 * P], start=True, stop=True)\
                  .then_inc(ctx_a_mm, 1)
                if b == 0:
                    pe.wait_ge(ctx_rep_ready, 1)
                pe.matmul(bank[2 + b][:, 0:3 * P], ctx_rep[:, b], wc_s[:, 0:3 * P], start=True, stop=True)\
                  .then_inc(ctx_b_mm, 1)
            pe.wait_ge(consts_ready, 3)
            for b in range(NB):
                pe.wait_ge(a_ready, b + 1)
                pe.wait_ge(a_ready_act, b + 1)
                transposes(bank[6 + b], a_n[:, b], a_tr)
                pe.wait_ge(ld_w0, 16)
                pe.wait_ge(a_f_ready, b + 1)
                pe.matmul(bank[6 + b][:], w0_s[:, 0:P], a_f[:, b], start=True, stop=True).then_inc(q0_mm, 1)
                pe.wait_ge(k0_ready, b + 1)
                pe.wait_ge(v0_ready, b + 1)
                o = bank[4 + b][:, 0:P + 1]
                pe.matmul(o, k0[:, b, 0], v0[:, b, 0], start=True, stop=False)
                pe.matmul(o, k0[0:KR, b, 1], v0[0:KR, b, 1], start=False, stop=True).then_inc(kv0_mm, 1)

            def numerator(b):
                pe.wait_ge(kv0_ready, b + 1)
                pe.wait_ge(q0_ready, b + 1)
                pe.matmul(bank[6 + b][:], kv0[:, b, 0:P], q0[:, b], start=True, stop=True).then_inc(num_mm, 1)
                if b == 0:
                    pe.wait_ge(ones_ready, 1)
                    pe.wait_ge(ld_row, 16)
                for j in range(NJ):
                    o = bank[4 + b][:, j * P:(j + 1) * P]
                    pe.matmul(o, a_f[:, b, j * P:(j + 1) * P], ident[:], start=j == 0, stop=False,
                              skip_group_check=True)
                    pe.matmul(o, ones_f[:], row[0:1, R_BO0:R_BO0 + P], start=False, stop=False,
                              skip_group_check=True)

            def project(b):
                pe.wait_ge(u_ready, b + 1)
                for j in range(NJ):
                    last = pe.matmul(bank[4 + b][:, j * P:(j + 1) * P], u_f[:, b, j * P:(j + 1) * P],
                                     w0_s[:, P:2 * P], start=False, stop=True, skip_group_check=True)
                last.then_inc(att0_mm, 1)

            numerator(0)
            pe.wait_ge(v1_ready, NB)
            pe.matmul(bank[0][:, 0:NB * TKP], wc_s[:, 3 * P:4 * P], ctx_t[:], start=True, stop=True)\
              .then_inc(k1_mm, 1)
            pe.wait_ge(ld_wf, 16)
            pe.wait_ge(ld_col, 16)
            for g in range(3):
                last = pe.matmul(bank[1][:, g:g + 1], wf_s[:, (3 + g) * P:(4 + g) * P], col[:, C_INC:C_INC + 1],
                                 start=True, stop=True)
            last.then_inc(gate_c_mm, 1)
            numerator(1)
            project(0)
            project(1)
            pe.wait_ge(k1_ready, 1)
            pe.wait_ge(gate_c_ready, 1)
            pe.wait_ge(z_ready, 1)
            pe.wait_ge(z_ready_act, 1)
            transposes(bank[6], z_n[:, 0], z_tr)
            for step in range(NB):
                pe.wait_ge(z_f_ready, step + 1)
                for g in range(3):
                    mm = pe.matmul(bank[3 * step + g][:], wf_s[:, g * P:(g + 1) * P], z_f[:, step],
                                   start=True, stop=step == 0)
                    if step == 0:
                        mm.then_inc(gates_mm, 1)
                        if g == 1:
                            pe.wait_ge(z_ready, 2)
                            pe.wait_ge(z_ready_act, 2)
                            transposes(bank[7], z_n[:, 1], z_tr)
            for b in range(NB):
                pe.wait_ge(gates_act, b + 1)
                pe.matmul(bank[b][:], wf_s[:, 6 * P:7 * P], z_f[:, b], start=True, stop=False)
            pe.wait_ge(cell_ready, 1)
            for g in range(3):
                pe.matmul(bank[3 + g][:], wf_s[:, (3 + g) * P:(4 + g) * P], cell[:, 0], start=False, stop=True)\
                  .then_inc(gates_mm, 1)
            pe.wait_ge(uo_ready, 1)
            pe.wait_ge(cell_ready, 2)
            for b in range(NB):
                pe.matmul(bank[b][:], uo_half[:], cell[:, 1], start=False, stop=True).then_inc(h_mm, 1)
            for b in range(NB):
                pe.wait_ge(h_act, b + 1)
                for j in range(NJ):
                    last = pe.transpose(bank[6 + b][:, j * P:(j + 1) * P], h_f[:, b, j * P:(j + 1) * P], ident[:])
                last.then_inc(h_tr, 1)
            pe.wait_ge(gates_act, 6)
            pe.wait_ge(ld_w3, 16)
            for b in range(NB):
                pe.wait_ge(s_ready, b + 1)
                pe.wait_ge(s_ready_act, b + 1)
                transposes(bank[2 + b], s_n[:, b], s_tr)
                pe.wait_ge(s_f_ready, b + 1)
                pe.matmul(bank[4 + b][:], w3_s[:, 0:P], s_f[:, b], start=True, stop=True).then_inc(q1_mm, 1)

            def scores(n):
                b, _, j, h0, nh = GROUPS[n]
                for i in range(nh):
                    last = pe.matmul(bank[bank_of(n)][:, i * TK:(i + 1) * TK],
                                     q_stack[BP * b:BP * b + ROWS_SCORE, h0 + i, j * P:(j + 1) * P],
                                     k_stack[BP * b:BP * b + ROWS_SCORE, h0 + i, 0:TK], start=True, stop=True)
                last.then_inc(score_mm, 1)

            def max_turn(b, k):
                pe.wait_ge(nm_parts, 2 * b + k + 1)
                nm_ps = bank[TB[ITEMS.index((b, k)) % 2]][0:3 * HALVES[k][1], 0:T // 2].bitcast(BF16)
                for j in range(NJ):
                    last = pe.transpose(nm_ps[:, j * P:(j + 1) * P], nm_part[k][:, b, j], ident_b[:])
                last.then_inc(nm_tr, 1)

            def item(i):
                if i >= 2:
                    before = ITEMS[i - 2]
                    if isinstance(before, tuple):
                        pe.wait_ge(nm_f_ready, 2 * before[0] + before[1] + 1)
                    else:
                        pe.wait_ge(max_taken, before + 1)
                it = ITEMS[i]
                if isinstance(it, tuple):
                    max_turn(*it)
                else:
                    if it == END[0][1]:
                        pe.wait_ge(q_stacked[1], 16 * (len(SLOTS) + 1))
                        pe.wait_ge(k_stacked[1], 16 * (len(SLOTS) + 2))
                    scores(it)

            def st(u):
                b, n = divmod(u, UPB)
                hq, i = UNITS[n]
                pe.wait_ge(nm_stacked[b][0], 16)
                if hq * HG + (i if i < HG else HG - 1) >= HALVES[1][0]:
                    pe.wait_ge(nm_stacked[b][1], 16)
                if u < 4:
                    pe.wait_ge(max_taken, END[0][0])
                else:
                    pe.wait_ge(prob_ready, u - 3)
                o = bank[RING[u % 4]]
                if i < HG:
                    last = pe.matmul(o[:], k_stack[BP * b:BP * b + ROWS_ALL, hq * HG + i, 0:P],
                                     q_stack[BP * b:BP * b + ROWS_ALL, hq * HG + i], start=True, stop=True)
                else:
                    for g in range(HG):
                        last = pe.matmul(o[KB * g:KB * g + KB], k_stack[BP * b:BP * b + ROWS_ALL, hq * HG + g, P:TKP],
                                         q_stack[BP * b:BP * b + ROWS_ALL, hq * HG + g], start=True, stop=True)
                last.then_inc(st_mm, 1)

            def pv(u):
                b, n = divmod(u, UPB)
                hq, i = UNITS[n]
                m = b * HQ + hq
                o = bank[PV[m % 2]]
                if u == 0:
                    pe.wait_ge(v_ready, 1)
                    pe.wait_ge(q_parts, 3 * NB)
                if i == 0 and m >= 2:
                    pe.wait_ge(o_ev_ready, m - 1)
                values = v_a[:, b, hq, i] if i < HG else v_b[:, b, hq]
                if hi_by(u) == "-":
                    pe.wait_ge(prob_ready, u + 1)
                    last = pe.matmul(o[:], values.bitcast(F32), prob[:, u % NPR], start=i == 0, stop=i == HG)
                else:
                    wait_both(pe, prob_hi_act, prob_hi_dve, hi_counts(u + 1))
                    wait_both(pe, prob_lo_pool, prob_lo_dve, p_lo_counts(u + 1))
                    for part in (prob_h, prob_l):
                        last = pe.matmul(o[:], values, part[:, u % NPR],
                                         start=i == 0 and part is prob_h, stop=i == HG and part is prob_l)
                last.then_inc(pv_mm, 1)

            def tail(b, piece):
                first, second = (bank[i] for i in TB)
                if piece <= T_NORM3:
                    hq = piece - T_NORM0
                    pe.wait_ge(o_ev_ready, b * HQ + hq + 1)
                    if b == 1 and hq < 3:
                        pe.wait_ge((o_f_ready, gap_ready, comb_f_ready)[hq], 1)
                    if b == 0 and hq == 0:
                        pe.wait_ge(max_taken, len(GROUPS))
                    if b == 0 and hq == 1:
                        pe.wait_ge(nm_f_ready, 2 * NB)
                    if hq >= 2:
                        pe.wait_ge(o_summed, b * HQ + hq - 1)
                    for j in range(NJ):
                        last = pe.transpose(bank[TB[hq % 2]][:, j * P:(j + 1) * P],
                                            o_ev[b][hq][:, j * P:(j + 1) * P], ident[:])
                    last.then_inc(o_turned, 1)
                elif piece == T_TURN:
                    pe.wait_ge(o_ready, b + 1)
                    transposes(first, o_t[:, b], o_tr)
                elif piece == T_PROJ:
                    pe.wait_ge(o_f_ready, b + 1)
                    for j in range(NJ):
                        last = pe.matmul(second[:, j * P:(j + 1) * P], o_f[:, b, j * P:(j + 1) * P],
                                         w3_s[:, P:2 * P], start=True, stop=True)
                    last.then_inc(att1_mm, 1)
                elif piece == T_IN:
                    pe.wait_ge(e_ready, b + 1)
                    pe.wait_ge(o_summed, HQ + 1)
                    transposes(first, e_n[:, b], e_tr)
                elif piece == T_GATE:
                    pe.wait_ge(e_f_ready, b + 1)
                    for j in range(NJ):
                        last = pe.matmul(second[:, j * E:(j + 1) * E], e_f[:, b, j * P:(j + 1) * P],
                                         w3_s[:, 2 * P:2 * P + E], start=True, stop=True)
                    last.then_inc(logit_mm, 1)
                elif piece == T_COMB:
                    pe.wait_ge(comb_ready, b + 1)
                    pe.wait_ge(e_l_ready, b + 1)
                    comb_ps = first[0:3 * E, 0:T // 2].bitcast(BF16)
                    for j in range(NJ):
                        last = pe.transpose(comb_ps[:, j * P:(j + 1) * P], comb_part[:, b, j], ident_b[:])
                    last.then_inc(comb_tr, 1)

            def comb_spread(n):
                b, e = divmod(n, E)
                if e == 0:
                    pe.wait_ge(comb_f_ready, b + 1)
                    pe.wait_ge(o_ev_ready, NB * HQ)
                else:
                    pe.wait_ge(comb_b_ready, n)
                pe.matmul(bank[XP[b][1]][:], pick_e[:, e], comb_f[:, b], start=True, stop=True)\
                  .then_inc(comb_b_mm, 1)

            def up(n):
                b, e = divmod(n, E)
                if e == 0:
                    pe.wait_ge(e_l_ready, b + 1)
                for c in range(HC):
                    g = n * HC + c
                    if g == 0:
                        pe.wait_ge(prob_ready, UNITS_ALL)
                        pe.wait_ge(w_lo, 8)
                    if g >= 4:
                        pe.wait_ge(hid_full, g - 3)
                    o = bank[RING[g % 4]][:]
                    wh, wl = w1_h[:, e, c * P:(c + 1) * P], w1_l[:, e, c * P:(c + 1) * P]
                    pe.matmul(o, wh, e_h[:, b], start=True, stop=False)
                    pe.matmul(o, wh, e_l[:, b], start=False, stop=False)
                    pe.matmul(o, wl, e_h[:, b], start=False, stop=True).then_inc(h1_mm, 1)

            def down(n):
                b, e = divmod(n, E)
                y = bank[XP[b][0]][:]
                if e == 0:
                    pe.wait_ge(b2_ready, 1)
                    for k in range(3):
                        pe.matmul(y, b2_part[:, k], comb_f[:, b], start=k == 0, stop=False)
                for c in range(HC):
                    g = n * HC + c
                    pe.wait_ge(hid_hi[c], n + 1)
                    n_pool, n_dve = lo_counts(g + 1)
                    pe.wait_ge(hid_lo_pool, n_pool)
                    if n_dve:
                        pe.wait_ge(hid_lo_dve, n_dve)
                    hh, hl = hid_h[:, g % NH], hid_l[:, g % NH]
                    pe.matmul(y, w2_h[:, e, c], hh, start=False, stop=False)
                    pe.matmul(y, w2_l[:, e, c], hh, start=False, stop=False)
                    last = pe.matmul(y, w2_h[:, e, c], hl, start=False, stop=e == E - 1 and c == HC - 1)
                last.then_inc(y_mm, 1)

            def y_turn(k):
                b, tiles, to = OUT[k]
                pe.wait_ge(y_f_ready, k + 1)
                for j in range(tiles.start, tiles.stop):
                    last = pe.transpose(bank[to][:, j * P:(j + 1) * P], y_f[:, b, j * P:(j + 1) * P], ident[:])
                last.then_inc(y_tr, 1)

            pe.wait_ge(q_stacked[0], 16 * (len(SLOTS) + 1))
            pe.wait_ge(k_stacked[0], 16 * (len(SLOTS) + 2))
            pe.wait_ge(x2_ready, NB)
            for n in range(END[0][0]):
                if n >= 4:
                    pe.wait_ge(max_taken, n - 3)
                scores(n)
            for u in range(-1, UNITS_ALL + LAG):
                if 0 <= u < UNITS_ALL:
                    st(u)
                if u == UNITS_ALL + 2:
                    up(0)
                if u >= LAG:
                    pv(u - LAG)
                if u < UNITS_ALL:
                    for i in items_after(u):
                        item(i)
                if u - UPB in UNIT_PE:
                    tail(*UNIT_PE[u - UPB])
            up(1)
            tail(1, T_NORM3)
            pe.wait_ge(w_lo, 8)
            comb_spread(0)
            for n in range(NB * E + 2):
                if 2 <= n < NB * E:
                    up(n)
                if n in TAIL_PE:
                    tail(1, TAIL_PE[n])
                if n >= 2:
                    down(n - 2)
                if n + 1 < NB * E:
                    comb_spread(n + 1)
                if n == E + 3:
                    y_turn(0)
            y_turn(1)
            y_turn(2)

        @block.vector
        def _(dve):
            steps = [0]

            def link(ins):
                steps[0] += 1
                ins.then_inc(dve_step, 1)
                dve.wait_ge(dve_step, steps[0])

            def ln_stats(n, b, src):
                for j in range(NJ):
                    last = dve.bn_stats(stats[:, n, b, j], src[:, j])
                link(last)
                for j in range(NJ):
                    last = dve.bn_aggr(mv[:, n, b, j], stats[:, n, b, j])
                link(last)
                dve.tensor_scalar(vare[:, n, b], mv[:, n, b, :, 1], EPS_LN, None, ALU.add).then_inc(var_ready, 1)
                dve.tensor_scalar(neg_mean[:, n, b], mv[:, n, b, :, 0], -1.0, None, ALU.mult).then_inc(mean_ready, 1)

            def ln_apply(n, b, src, dst, tiles=NJ):
                dve.wait_ge(rstd_ready, n * NB + b + 1)
                for j in range(tiles):
                    last = dve.scalar_tensor_tensor(out=dst[:, b, j], in0=src[:, b, j], scalar=mv[:, n, b, j, 0:1],
                                                    in1=rstd[:, n, b, j:j + 1].broadcast_to([P, P]),
                                                    op0=ALU.subtract, op1=ALU.mult)
                return last

            def by_tile(ap):
                return ap.rearrange("p (j d) -> p j d", j=NJ)

            dve.memset(ctx_t[:, :, TK:TKP], 0.0).then_inc(pad_ready, 1)

            dve.memset(eps_den[:], EPS_DEN).then_inc(eps_ready, 1)
            dve.memset(v0[:, :, :, P:P + 1], 1.0)
            dve.memset(ones_b[:], 1.0)
            link(dve.memset(mask_b[:], MASKED))
            link(dve.memset(v_a[:].bitcast(F32), 0.0))
            dve.wait_ge(ld_x[0], 16)
            ln_stats(LN_X, 0, x_t[:, 0])
            dve.wait_ge(ld_ctx, 32)
            for g in range(HG):
                last = dve.tensor_copy(ctx_rep[:, :, g], ctx_t[:, :, P:TKP])
            last.then_inc(ctx_rep_ready, 1)
            dve.wait_ge(ld_x[1], 16)
            ln_stats(LN_X, 1, x_t[:, 1])
            dve.wait_ge(ld_col, 16)
            dve.tensor_scalar(bq0_1[:], col[:, C_BQ0:C_BQ0 + 1], 1.0, None, ALU.add)
            dve.tensor_scalar(bq0_neg[:], col[:, C_BQ0:C_BQ0 + 1], -1.0, None, ALU.mult).then_inc(bq0_ready, 1)
            link(dve.memset(v_b[:].bitcast(F32), 0.0))
            for g in range(HG):
                dve.memset(v_a[:, :, :, g, GW * g + HD:GW * g + HD + 1].bitcast(F32), 1.0)
                last = dve.memset(v_b[KB * g:KB * g + KB, :, :, GW * g + HD:GW * g + HD + 1].bitcast(F32), 1.0)
            last.then_inc(v_pad, 1)
            dve.wait_ge(ld_mask, 16)
            dve.tensor_scalar(mask_b[:, :, 0:TK], mask_u[:, :, 0:TK], MASKED, None, ALU.mult)\
               .then_inc(mask_ready, 1)
            dve.wait_ge(ld_row, 16)

            def keys_values(b):
                dve.wait_ge(ctx_a_mm, b + 1)
                dve.tensor_tensor(k0_b[:, b, 0], bank[b][:, 0:P], row[:, R_BK0:R_BK0 + P], ALU.add)
                dve.wait_ge(ctx_b_mm, b + 1)
                link(dve.tensor_tensor(k0_b[:, b, 1], bank[2 + b][:, 0:P], row[:, R_BK0:R_BK0 + P], ALU.add))
                dve.tensor_scalar(k0_m[:, b], k0_b[:, b], 0.0, None, ALU.min).then_inc(k0_neg, 1)
                dve.tensor_tensor(v0[:, b, 0, 0:P], bank[b][:, P:2 * P], row[:, R_BV0:R_BV0 + P], ALU.add)
                dve.tensor_tensor(v0[:, b, 1, 0:P], bank[2 + b][:, P:2 * P], row[:, R_BV0:R_BV0 + P],
                                  ALU.add).then_inc(v0_ready, 1)

            def keys_phi(b):
                dve.wait_ge(k0_exp, b + 1)
                dve.scalar_tensor_tensor(out=k0[:, b], in0=k0_b[:, b], scalar=1.0, in1=k0_e[:, b],
                                         op0=ALU.add, op1=ALU.max).then_inc(k0_ready, 1)

            def state(b):
                dve.wait_ge(kv0_mm, b + 1)
                dve.tensor_copy(kv0[:, b], bank[4 + b][:, 0:P + 1]).then_inc(kv0_ready, 1)

            def queries_phi(b):
                dve.wait_ge(q0_exp, b + 1)
                dve.scalar_tensor_tensor(out=q0[:, b], in0=bank[6 + b][:], scalar=bq0_1[:], in1=q_e[:, b],
                                         op0=ALU.add, op1=ALU.max).then_inc(q0_ready, 1)

            def reciprocal(b):
                dve.wait_ge(den_ready, b + 1)
                dve.reciprocal(rden[:, b], den[:, b]).then_inc(rden_ready, 1)

            def quotient(b):
                dve.wait_ge(rden_ready, b + 1)
                dve.wait_ge(num_mm, b + 1)
                dve.tensor_tensor(u_f[:, b], bank[6 + b][:], rden[:, b], ALU.mult).then_inc(u_ready, 1)

            for b in range(NB):
                ln_apply(LN_X, b, x_t, a_n, NJ_DVE).then_inc(a_ready, 1)
            keys_values(0)
            keys_phi(0)
            keys_values(1)
            queries_phi(0)
            state(0)
            keys_phi(1)
            state(1)
            reciprocal(0)
            queries_phi(1)
            quotient(0)
            reciprocal(1)
            quotient(1)
            dve.wait_ge(gate_c_mm, 1)
            dve.tensor_tensor(gate0[:, 2:3], bank[1][:, 2:3], col[:, C_BC:C_BC + 1], ALU.add)
            dve.tensor_scalar(gate0[:, 0:1], bank[1][:, 0:1], col[:, C_BF:C_BF + 1], 0.5, ALU.add, ALU.mult)
            dve.tensor_scalar(gate0[:, 1:2], bank[1][:, 1:2], col[:, C_BI:C_BI + 1], 0.5, ALU.add, ALU.mult)
            dve.tensor_scalar(gate1[:, 0:2], col[:, C_BF:C_BF + 2], 0.5, None, ALU.mult)
            dve.tensor_copy(gate1[:, 2:3], col[:, C_BC:C_BC + 1])
            dve.tensor_scalar(c0_half[:], col[:, C_INC:C_INC + 1], 0.5, None, ALU.mult).then_inc(gate_c_ready, 1)
            for b in range(NB):
                dve.wait_ge(att0_mm, b + 1)
                ln_stats(LN_R, b, by_tile(bank[4 + b][:]))
            gamma = row[:, R_GAMMA:R_GAMMA + P].rearrange("p (o d) -> p o d", o=1).broadcast_to([P, NJ, P])
            for j in range(NJ):
                last = dve.scalar_tensor_tensor(out=r_t[:, 0, j], in0=bank[4][:, j * P:(j + 1) * P],
                                                scalar=mv[:, LN_R, 0, j, 0:1], in1=gamma[:, j],
                                                op0=ALU.subtract, op1=ALU.mult)
            link(last)
            dve.wait_ge(rstd_ready, LN_R * NB + 1)
            dve.wait_ge(x_beta_ready, 1)
            for j in range(NJ):
                last = dve.scalar_tensor_tensor(out=x1[:, 0, j], in0=r_t[:, 0, j],
                                                scalar=rstd[:, LN_R, 0, j:j + 1], in1=x_beta[:, 0, j],
                                                op0=ALU.mult, op1=ALU.add)
            link(last)
            ln_stats(LN_X1, 0, x1[:, 0])
            dve.wait_ge(y_ready, 1)
            link(dve.tensor_tensor(r_t[:, 1], y_t[:, 1], gamma, ALU.mult))
            dve.wait_ge(x_beta_ready, 2)
            link(dve.tensor_tensor(x1[:, 1], r_t[:, 1], x_beta[:, 1], ALU.add))
            ln_stats(LN_X1, 1, x1[:, 1])
            for b in range(NB):
                ln_apply(LN_X1, b, x1, z_n, NJ_DVE).then_inc(z_ready, 1)
            for step in range(NB):
                dve.wait_ge(gates_act, 3 * step + 1)
                if step == 0:
                    dve.tensor_scalar(g_f[:, 0], g_act[:, 0, 0], 1.0, c0_half[:], ALU.add, ALU.mult)
                else:
                    dve.scalar_tensor_tensor(out=g_f[:, 1], in0=g_act[:, 1, 0], scalar=1.0, in1=cell[:, 0],
                                             op0=ALU.add, op1=ALU.mult)
                dve.wait_ge(gates_act, 3 * step + 3)
                link(dve.scalar_tensor_tensor(out=g_i[:, step], in0=g_act[:, step, 1], scalar=1.0,
                                              in1=g_act[:, step, 2], op0=ALU.add, op1=ALU.mult))
                dve.scalar_tensor_tensor(out=cell[:, step], in0=g_i[:, step], scalar=0.5 if step == 0 else 1.0,
                                         in1=g_f[:, step], op0=ALU.mult, op1=ALU.add).then_inc(cell_ready, 1)
                dve.wait_ge(cell_ready, step + 1)
            for b in range(NB):
                dve.wait_ge(h_tr, b + 1)
                dve.tensor_tensor(x2[:, b], by_tile(bank[6 + b][:]), x1[:, b], ALU.add).then_inc(x2_ready, 1)
                dve.wait_ge(x2_ready, b + 1)
                ln_stats(LN_X2, b, x2[:, b])
            for b in range(NB):
                ln_apply(LN_X2, b, x2, s_n, NJ_DVE).then_inc(s_ready, 1)
            for b in range(NB):
                dve.wait_ge(q1_mm, b + 1)
                link(dve.tensor_scalar(q1[:, b], bank[4 + b][:], col[:, C_BQ1:C_BQ1 + 1], QK_SCALE, ALU.add,
                                       ALU.mult))
                dve.tensor_copy(q_part[:, b, 0], q1[:, b]).then_inc(q_parts, 1)
                dve.wait_ge(q_parts, 3 * b + 1)
                link(dve.tensor_tensor(q_r1[:, b], q1[:, b], q_part[:, b, 0], ALU.subtract))
                dve.tensor_copy(q_part[:, b, 1], q_r1[:, b]).then_inc(q_parts, 1)
                dve.wait_ge(q_parts, 3 * b + 2)
                dve.tensor_tensor(q_part[:, b, 2], q_r1[:, b], q_part[:, b, 1], ALU.subtract).then_inc(q_parts, 1)

            def maximum(n):
                b, k, j, h0, nh = GROUPS[n]
                dve.wait_ge(score_mm, n + 1)
                src = bank[bank_of(n)][:, 0:nh * TK]
                dve.tensor_reduce(nmax[:, b, j, h0:h0 + nh], src.rearrange("p (h k) -> p h k", k=TK),
                                  AX.X, ALU.max, negate=True).then_inc(max_taken, 1)
                if n + 1 == END[b][k]:
                    h0, nh = HALVES[k]
                    whole, rest, part = nmax[:, b, :, h0:h0 + nh], nm_r1[:, b, :, h0:h0 + nh], nm_part[k][:, b]
                    dve.wait_ge(max_taken, n + 1)
                    link(dve.tensor_copy(part[:, :, 0], whole))
                    link(dve.tensor_tensor(rest, whole, part[:, :, 0], ALU.subtract))
                    link(dve.tensor_copy(part[:, :, 1], rest))
                    dve.tensor_tensor(part[:, :, 2], rest, part[:, :, 1], ALU.subtract).then_inc(nm_parts, 1)

            def prob_hi(u):
                if hi_by(u) == "D":
                    dve.wait_ge(prob_ready, u + 1)
                    if u >= NPR:
                        dve.wait_ge(pv_mm, u - NPR + 1)
                    dve.tensor_copy(prob_h[:, u % NPR], prob[:, u % NPR]).then_inc(prob_hi_dve, 1)

            def prob_lo(u):
                if lo_by(u) == "D":
                    n_act, n_dve = hi_counts(u + 1)
                    if hi_by(u) == "A":
                        dve.wait_ge(prob_hi_act, n_act)
                    else:
                        dve.wait_ge(prob_hi_dve, n_dve)
                    if u >= NPR:
                        dve.wait_ge(pv_mm, u - NPR + 1)
                    dve.tensor_tensor(prob_l[:, u % NPR], prob[:, u % NPR], prob_h[:, u % NPR].bitcast(F32),
                                      ALU.subtract).then_inc(prob_lo_dve, 1)

            def tail(b, piece):
                first, second = (bank[i] for i in TB)
                if piece <= T_NORM3:
                    hq = piece - T_NORM0
                    dve.wait_ge(o_turned, b * HQ + hq + 1)
                    view = bank[TB[hq % 2]][:].rearrange("p (n c) -> p n c", c=GW)
                    dve.tensor_copy(o_sum[:, b, hq], view[:, :, HD + 1:2 * HD + 1])
                    link(dve.reciprocal(rsum[:, b, hq], view[:, :, HD]))
                    dve.tensor_tensor(o_sum[:, b, hq], view[:, :, 0:HD], o_sum[:, b, hq], ALU.add)\
                       .then_inc(o_summed, 1)
                    dve.wait_ge(o_summed, b * HQ + hq + 1)
                    f = slice(hq * HG * HD, (hq + 1) * HG * HD)
                    dve.tensor_tensor(o_t[:, b, :, f].rearrange("p j (g d) -> p j g d", d=HD),
                                      o_sum[:, b, hq].rearrange("p (j g) d -> p j g d", j=NJ),
                                      rsum[:, b, hq].rearrange("p (j g o) -> p j g o", j=NJ, o=1)
                                      .broadcast_to([P, NJ, HG, HD]), ALU.mult).then_inc(o_normed, 1)
                    if piece == T_NORM3:
                        dve.wait_ge(o_normed, (b + 1) * HQ)
                        dve.memset(o_done[:], 0.0).then_inc(o_ready, 1)
                elif piece == T_PROJ:
                    dve.wait_ge(att1_mm, b + 1)
                    dve.wait_ge(x2_bo_ready, b + 1)
                    dve.tensor_tensor(x3[:, b], by_tile(second[:]), x2_bo[:, b], ALU.add).then_inc(x3_ready, 1)
                    dve.wait_ge(x3_ready, b + 1)
                    ln_stats(LN_X3, b, x3[:, b])
                elif piece == T_IN:
                    ln_apply(LN_X3, b, x3, e_n).then_inc(e_ready, 1)
                elif piece == T_GATE:
                    dve.wait_ge(e_f_ready, b + 1)
                    dve.tensor_tensor(e_l[:, b], first[:], e_h[:, b].bitcast(F32), ALU.subtract)\
                       .then_inc(e_l_ready, 1)
                    dve.wait_ge(logit_mm, b + 1)
                    bg = row[:, R_BG:R_BG + E].rearrange("p (o e) -> p o e", o=1).broadcast_to([P, NJ, E])
                    link(dve.tensor_tensor(logit[:, b], second[:, 0:NJ * E].rearrange("p (j e) -> p j e", j=NJ),
                                           bg, ALU.add))
                    for j in range(NJ):
                        last = dve.max(top_v[:, b, j], logit[:, b, j])
                    link(last)
                    dve.tensor_tensor(gap[:, b], top_v[:, b, :, 1], top_v[:, b, :, 0], ALU.subtract)\
                       .then_inc(gap_ready, 1)
                    for j in range(NJ):
                        last = dve.max_index(top_i[:, b, j], top_v[:, b, j], logit[:, b, j])
                    link(last)
                    dve.tensor_copy(top_f[:, b], top_i[:, b]).then_inc(top_ready, 1)
                elif piece == T_PICK:
                    dve.wait_ge(top_ready, b + 1)
                    iota = iota_f[:].rearrange("p (o e) -> p o e", o=1).broadcast_to([P, NJ, E])

                    def pick(k):
                        return top_f[:, b, :, k:k + 1].broadcast_to([P, NJ, E])

                    def weight(k):
                        return w_top[:, b, k].rearrange("p (j o) -> p j o", o=1).broadcast_to([P, NJ, E])

                    dve.tensor_tensor(hit1[:, b], iota, pick(0), ALU.is_equal)
                    dve.tensor_tensor(hit2[:, b], iota, pick(1), ALU.is_equal)
                    dve.wait_ge(gap_exp, b + 1)
                    link(dve.tensor_scalar(gap_1[:, b], gap_e[:, b], 1.0, None, ALU.add))
                    link(dve.reciprocal(w_top[:, b, 0], gap_1[:, b]))
                    link(dve.tensor_tensor(w_top[:, b, 1], w_top[:, b, 0], gap_e[:, b], ALU.mult))
                    dve.tensor_tensor(hit1w[:, b], hit1[:, b], weight(0), ALU.mult)
                    link(dve.tensor_tensor(hit2w[:, b], hit2[:, b], weight(1), ALU.mult))
                    link(dve.tensor_tensor(comb[:, b], hit1w[:, b], hit2w[:, b], ALU.add))
                    link(dve.tensor_copy(comb_part[:, b, :, 0], comb[:, b]))
                    link(dve.tensor_tensor(comb_r[:, b], comb[:, b], comb_part[:, b, :, 0], ALU.subtract))
                    link(dve.tensor_copy(comb_part[:, b, :, 1], comb_r[:, b]))
                    dve.tensor_tensor(comb_part[:, b, :, 2], comb_r[:, b], comb_part[:, b, :, 1],
                                      ALU.subtract).then_inc(comb_ready, 1)

            def hidden(n):
                for c in range(HC):
                    g = n * HC + c
                    h = hid[:, g % NH]
                    dve.wait_ge(hid_full, g + 1)
                    dve.wait_ge(comb_b_ready, n + 1)
                    dve.tensor_tensor(h, h, comb_b[:, n % NCB], ALU.mult).then_inc(weighted, 1)
                    if c == 0:
                        dve.wait_ge(weighted, g + 1)
                        dve.tensor_copy(hid_h[:, g % NH], h).then_inc(hid_hi[0], 1)

            def hidden_lo(n):
                for c in range(HC):
                    if not lo_on_pool(n, c):
                        g = n * HC + c
                        dve.wait_ge(hid_hi[c], n + 1)
                        dve.tensor_tensor(hid_l[:, g % NH], hid[:, g % NH], hid_h[:, g % NH].bitcast(F32),
                                          ALU.subtract).then_inc(hid_lo_dve, 1)

            def finish(k):
                b, tiles, to = OUT[k]
                dve.wait_ge(y_tr, k + 1)
                dve.tensor_tensor(res[:, b, tiles], by_tile(bank[to][:])[:, tiles], x3[:, b, tiles], ALU.add)\
                   .then_inc(res_ready, 1)

            dve.tensor_copy(iota_f[:], iota_u[:])
            for n in range(END[0][0]):
                maximum(n)
            for u in range(-1, UNITS_ALL + LAG):
                if 0 <= u < UNITS_ALL:
                    prob_hi(u)
                if 1 <= u <= UNITS_ALL:
                    prob_lo(u - 1)
                if u < UNITS_ALL:
                    for i in items_after(u):
                        if not isinstance(ITEMS[i], tuple):
                            maximum(ITEMS[i])
                if u - UPB in UNIT_DVE:
                    tail(*UNIT_DVE[u - UPB])
            tail(1, T_NORM3)
            for n in range(NB * E + 1):
                if n < NB * E:
                    hidden(n)
                if n >= 1:
                    hidden_lo(n - 1)
                if n in TAIL_DVE:
                    tail(1, TAIL_DVE[n])
                if n == E + 3:
                    finish(0)
            finish(1)
            finish(2)


def kernel(**inputs):
    import numpy as np
    import concourse.bacc as bacc
    from concourse.bass_utils import run_bass_kernel_spmd

    a = {k: np.asarray(v) for k, v in inputs.items()}

    def by_feature(m):
        return m.reshape(m.shape[:-1] + (H, HD)).swapaxes(-1, -2).reshape(m.shape)

    wk1, wv1 = a["L1_xattn_Wkv"][:, :P], a["L1_xattn_Wkv"][:, P:]
    bk1, bv1 = a["L1_xattn_bkv"][:P], a["L1_xattn_bkv"][P:]
    b1 = a["L1_ffn_b1"].reshape(E * HC, P)
    laid = {
        "x": a["x"],
        "ctxt": a["ctx_1024"].transpose(2, 0, 1),
        "mask": a["mask_BxS2_bk0"][None],
        "w_ctx": np.concatenate([a["L0_xattn_Wk"].T, a["L0_xattn_Wv"].T, wv1, by_feature(wk1)], axis=1),
        "w_l0": np.concatenate([a["L0_xattn_Wq"].T, a["L0_xattn_Wo"].T], axis=1),
        "w_ffn": np.concatenate([a["L0_ffn_" + n].T for n in W_FFN], axis=1),
        "w_l1": np.concatenate([by_feature(a["L1_xattn_Wq"]), a["L1_xattn_Wo"], a["L1_ffn_Wg"]], axis=1),
        "cols": np.stack([a["L0_xattn_bq"], a["L0_ffn_bf"], a["L0_ffn_bi"], a["L0_ffn_bc"], a["L0_ffn_in_c"],
                          a["L0_ffn_bo"], by_feature(bk1), by_feature(a["L1_xattn_bq"]), *b1], axis=1),
        "rows": np.concatenate([a["L0_xattn_bo"], a["L0_xattn_gamma"], a["L0_xattn_beta"], a["L1_xattn_bo"],
                                a["L1_ffn_bg"], a["L0_xattn_bk"], a["L0_xattn_bv"], bv1]),
        "w1": a["L1_ffn_W1"],
        "w2": a["L1_ffn_W2"],
        "b2": a["L1_ffn_b2"],
    }
    nc = bacc.Bacc("TRN2", target_bir_lowering=False, num_devices=1)
    arrays, args = {}, []
    for name, v in laid.items():
        v = np.ascontiguousarray(v)
        arrays[f"in_{name}"] = v
        args.append(nc.dram_tensor(f"in_{name}", v.shape, mybir.dt.from_np(v.dtype), kind="ExternalInput").ap())
    args.append(nc.dram_tensor("out_x", (NB, T, P), F32, kind="ExternalOutput").ap())
    two_blocks(nc, *args)
    r = run_bass_kernel_spmd(nc, [arrays], core_ids=[0])
    return r.results[0]["out_x"]
```
